# Optimizing a Trainium2 kernel written in Bass

```python
import numpy as np
import jax
import jax.numpy as jnp

def _softmax(x, axis=-1):
    return jax.nn.softmax(x, axis=axis)
def _gelu(x):
    return jax.nn.gelu(x, approximate=True)
def _silu(x):
    return jax.nn.silu(x)
def _sigmoid(x):
    return jax.nn.sigmoid(x)
def _layernorm(x, axis=-1, eps=1e-5):
    m = jnp.mean(x, axis=axis, keepdims=True)
    v = jnp.var(x, axis=axis, keepdims=True)
    return (x - m) / jnp.sqrt(v + eps)
def _scatter_add(tgt, idx, src, axis=0):
    return tgt.at[idx].add(src)
def _segment_sum(src, seg, n):
    return jax.ops.segment_sum(src, seg, n)

kernel_name = 'mk_conv_preact_d1_conv_nchw256_3b7cc1'

def setup_inputs(seed: int = 0):
    np.random.seed(seed)
    _w = jnp.asarray
    def _rec_inputs():
        import jax
        import jax.numpy as jnp
        _gk = jax.random.key(seed)
        x = -0.0003957 + 1 * jax.random.normal(jax.random.fold_in(_gk, 1), (16, 256, 56, 56), jnp.float32)
        return x
    x = _rec_inputs()
    def _L0_conv_setup():
        import jax, jax.numpy as jnp
        import numpy as np
        from jax import lax
        EPS = 0.0001
        K, STRIDE, PAD = (3, 1, 1)

        def _conv_nchw(x, w, stride, pad):
            return lax.conv_general_dilated(x, w, window_strides=(stride, stride), padding=[(pad, pad), (pad, pad)], dimension_numbers=('NCHW', 'OIHW', 'NCHW'))
        key = jax.random.key(seed)
        ks = jax.random.split(key, 6)
        N, C, H, W = (16, 256, 56, 56)
        Cout = 256
        return {'x': jax.random.normal(ks[0], (N, C, H, W), jnp.float32), 'bn_gamma': jax.random.uniform(ks[1], (C,), jnp.float32, 0.5, 1.5), 'bn_beta': jax.random.normal(ks[2], (C,), jnp.float32) * 0.1, 'conv_w': jax.random.normal(ks[3], (Cout, C, K, K), jnp.float32) * (1.0 / np.sqrt(C * K * K)), 'conv_b': jax.random.normal(ks[4], (Cout,), jnp.float32) * 0.01, 'beta_conv_b': jax.random.normal(ks[5], (1,), jnp.float32) * 0.01}
    _L0_conv_all = _L0_conv_setup()
    _L0_conv_in = {k: v for k, v in _L0_conv_all.items() if k in ('bn_gamma', 'bn_beta', 'conv_w', 'conv_b', 'beta_conv_b', )}
    del _L0_conv_all

    return {
        "x": x,
        "L0_conv_bn_gamma": _L0_conv_in["bn_gamma"],
        "L0_conv_bn_beta": _L0_conv_in["bn_beta"],
        "L0_conv_conv_w": _L0_conv_in["conv_w"],
        "L0_conv_conv_b": _L0_conv_in["conv_b"],
        "L0_conv_beta_conv_b": _L0_conv_in["beta_conv_b"],
    }

def reference(x, L0_conv_bn_gamma, L0_conv_bn_beta, L0_conv_conv_w, L0_conv_conv_b, L0_conv_beta_conv_b):
    import jax
    import jax.numpy as jnp
    def _L0_conv_ref(x, bn_gamma, bn_beta, conv_w, conv_b, beta_conv_b):
        import jax, jax.numpy as jnp
        import numpy as np
        from jax import lax
        EPS = 0.0001
        K, STRIDE, PAD = (3, 1, 1)

        def _conv_nchw(x, w, stride, pad):
            return lax.conv_general_dilated(x, w, window_strides=(stride, stride), padding=[(pad, pad), (pad, pad)], dimension_numbers=('NCHW', 'OIHW', 'NCHW'))
        mean = jnp.mean(x, axis=(0, 2, 3), keepdims=True)
        var = jnp.mean(jnp.square(x - mean), axis=(0, 2, 3), keepdims=True)
        xn = (x - mean) * lax.rsqrt(var + EPS)
        xn = xn * bn_gamma[None, :, None, None] + bn_beta[None, :, None, None]
        t = jnp.where(xn >= 0.0, 1.0, 0.0)
        t = jnp.where(xn <= 0.0, -1.0, t).astype(xn.dtype)
        xc = jnp.clip(xn, -1.0, 1.0)
        c_sum = jnp.sum(xc * t, axis=1, keepdims=True)
        c_cnt = jnp.sum(jnp.abs(t), axis=1, keepdims=True)
        y = _conv_nchw(t, conv_w, STRIDE, PAD) + conv_b[None, :, None, None]
        ones_k = jnp.ones((1, 1, K, K), x.dtype)
        b_sum = _conv_nchw(c_sum, ones_k, STRIDE, PAD) + beta_conv_b[0]
        b_cnt = _conv_nchw(c_cnt, ones_k, STRIDE, PAD) + beta_conv_b[0]
        beta_map = b_sum / b_cnt
        return y * beta_map

    def _gn(v, G=32, eps=1e-5):
        B_, C_, H_, W_ = v.shape
        g = v.reshape(B_, G, C_ // G, H_, W_)
        m = jnp.mean(g, axis=(2, 3, 4), keepdims=True)
        s = jnp.var(g, axis=(2, 3, 4), keepdims=True)
        return ((g - m) / jnp.sqrt(s + eps)).reshape(v.shape)

    def _ln_c(v, eps=1e-6):
        m = jnp.mean(v, axis=1, keepdims=True)
        s = jnp.var(v, axis=1, keepdims=True)
        return (v - m) / jnp.sqrt(s + eps)

    def _ln_t(v, eps=1e-5):
        m = jnp.mean(v, axis=-1, keepdims=True)
        s = jnp.var(v, axis=-1, keepdims=True)
        return (v - m) / jnp.sqrt(s + eps)

    def _to_tokens(v):
        B_, C_, H_, W_ = v.shape
        return v.reshape(B_, C_, H_ * W_).transpose(0, 2, 1)
    def _from_tokens(t, like):
        B_, C_, H_, W_ = like.shape
        return t.transpose(0, 2, 1).reshape(B_, C_, H_, W_)

    x = x + _L0_conv_ref(_gn(x), L0_conv_bn_gamma, L0_conv_bn_beta, L0_conv_conv_w, L0_conv_conv_b, L0_conv_beta_conv_b)
    return x


_drawn_inputs = setup_inputs


def setup_inputs(seed=0):
    import zlib

    import numpy as np

    out = dict(_drawn_inputs(seed))
    spreads = {}
    factors = {'L0_conv_conv_b': 8.0}
    for name, (base, spread) in spreads.items():
        noise = np.random.default_rng([zlib.crc32(name.encode()), seed]).standard_normal(out[name].shape)
        drawn = base * np.exp(spread * noise) if base else spread * noise
        out[name] = jnp.asarray(drawn.astype(out[name].dtype))
    for name, factor in factors.items():
        out[name] = (out[name] * factor).astype(out[name].dtype)
    return out
```

```python
from contextlib import ExitStack

import concourse.bass as bass
from concourse import mybir

F32 = mybir.dt.float32
F16 = mybir.dt.float16
U32 = mybir.dt.uint32
ALU = mybir.AluOpType
ACT = mybir.ActivationFunctionType
AX = mybir.AxisListType

P = 128
NI, C, H, W = 16, 256, 56, 56
CT = C // P
HR = H // 2
HPX = HR * W
J = W // 4
N = HR * J
K6 = 6
G4 = 2 * CT
UP = 60
GROUP = 8
GN_EPS, BN_EPS = 1e-5, 1e-4
SROWS = 7
SN = SROWS * W
SCH = HPX // SN
VPLANE = {0: 0, 5: 1, 1: 2, 2: 3, 3: 4, 4: 5}
BANKS = (1, 3, 2, 4, 0, 5)
C_GROUP, C_SEL, C_TRI, C_COUNT = 0, P, P + 15, P + 15 + P
C_WIDTH = C_COUNT + W


def conv_preact(nc, x, w_t, gamma, beta, conv_b, beta_b, consts, map_rows, out):
    x_v = x.rearrange("n (c p) (h r) w -> n c h p (r w)", p=P, h=2)
    out_v = out.rearrange("n (c p) (h r) w -> n c h p (r w)", p=P, h=2)
    x_pairs = x_v[1:NI - 1].rearrange("(i k) c h p f -> i k c h p f", k=2)
    w_v = w_t.rearrange("(c p) t o -> p c (t o)", p=P)

    with ExitStack() as ctx:
        def sb(name, shape, dt=F32):
            return ctx.enter_context(nc.sbuf_tensor(name, shape, dt))

        def sem(name):
            return ctx.enter_context(nc.semaphore(name))

        xb = sb("xb", [P, 2, G4, HPX])
        U = sb("U", [P, CT, 2, K6, 3, C], F16)
        V = sb("V", [P, 2, CT, K6, (H + 2) * J], F16)
        u = sb("u", [P, HR, UP], F16)
        T = sb("T", [P, K6, N], F16)
        T4 = sb("T4", [P, 4, N], F16)
        cq = sb("cq", [P, 4, N], F16)
        aq = sb("aq", [P, 2, N], F16)
        r = sb("r", [P, CT, HPX])
        ssum = sb("ssum", [P, HPX])
        shi = sb("shi", [P, HPX], F16)
        slo = sb("slo", [P, HPX], F16)
        sel = sb("sel", [P, 15], F16)
        bmap = sb("bmap", [P, 2, HPX])
        m13 = sb("m13", [P, 2, N])
        sd = sb("sd", [P, 4, N])
        y = sb("y", [P, 2, 4, N])
        cs8 = sb("cs8", [2 * SCH, SN])
        crow = sb("crow", [H, W + 2])
        hsum = sb("hsum", [H, 2, W])
        bm = sb("bm", [H, 4, J])
        rcount = sb("rcount", [H, W])
        cst = sb("cst", [P, C_WIDTH])
        vec = sb("vec", [P, 3, CT])
        bb = sb("bb", [P, 1])
        one = sb("one", [1, 1])
        mxb = sb("mxb", [P, C])
        scl = sb("scl", [P, C])
        inv_s = sb("inv_s", [P, CT])
        neg_inv = sb("neg_inv", [P, CT])
        st = sb("st", [P, 2, CT, 8, 6])
        mark = sb("mark", [P, 2, CT])
        mvt = sb("mvt", [P, 2, CT, 2])
        mv = sb("mv", [P, NI, CT, 2])
        tmp = sb("tmp", [P, 8, NI * CT])
        bnv = sb("bnv", [P, 8, CT])
        AB = sb("AB", [P, NI, 3, CT])
        ab = sb("ab", [P, 2, 3, CT])
        scratch = V[:, :, :, :, :].rearrange("p a c k n -> p (a c k n)").bitcast(F32)
        wt = scratch[:, 0:CT * 9 * C].rearrange("p (c a b o) -> p c a b o", c=CT, a=3, b=3)
        wtmp = scratch[:, CT * 9 * C:CT * 9 * C + 6 * 3 * C].rearrange("p (k a o) -> p k a o", k=6, a=3)

        acc = ctx.enter_context(nc.psum_tensor("acc", [P, K6, 512], F32))
        csum = ctx.enter_context(nc.psum_tensor("csum", [P, 512], F32))
        box = ctx.enter_context(nc.psum_tensor("box", [P, 512], F32))

        w_in, vec_in, cst_in = sem("w_in"), sem("vec_in"), sem("cst_in")
        x_in = [[sem(f"x_in{a}{g}") for g in range(G4)] for a in range(2)]
        x_out = [[sem(f"x_out{a}{g}") for g in range(G4)] for a in range(2)]
        stats_read, aggr_done, mv_done = sem("stats_read"), sem("aggr_done"), sem("mv_done")
        wmax, wall, wrow, wscale = sem("wmax"), sem("wall"), sem("wrow"), sem("wscale")
        w_pool, w_act, scale_ready = sem("w_pool"), sem("w_act"), sem("scale_ready")
        step, mean_ready, grp = sem("step"), sem("mean_ready"), sem("grp")
        root_in, root_out, coef_ready = sem("root_in"), sem("root_out"), sem("coef_ready")
        pads, weights_ready = sem("pads"), sem("weights_ready")
        ab_ready, u_ready, t_ready, cq_done, aq_done, v_ready = (
            sem(s) for s in ("ab_ready", "u_ready", "t_ready", "cq_done", "aq_done", "v_ready"))
        hi_ready, lo_ready = sem("hi_ready"), sem("lo_ready")
        abs_done, q_ready, s_ready, cs_done, cs8_ready, crow_in = (
            sem(s) for s in ("abs_done", "q_ready", "s_ready", "cs_done", "cs8_ready", "crow_in"))
        hpart, hsum_ready, box_done, bm_ready, bm_stored = (
            sem(s) for s in ("hpart", "hsum_ready", "box_done", "bm_ready", "bm_stored"))
        bmap_in = [sem(f"bmap_in{h}") for h in range(2)]
        m13_done, m24_done, m05_done, ev13, sd_done, y05_done, y_done, scaled, added = (
            sem(s) for s in ("m13_done", "m24_done", "m05_done", "ev13", "sd_done", "y05_done",
                             "y_done", "scaled", "added"))

        WA = 12
        WP = 15
        STAT_LOADS = 16 * (NI // 2)

        def arrived(n, parity):
            return STAT_LOADS + 8 * (n - parity)

        def at_least(eng, s, value):
            if not (isinstance(value, int) and value <= 0):
                eng.wait_ge(s, value)

        block = ctx.enter_context(nc.Block())

        @block.sync
        def _(sp):
            def stat_loads(i, even):
                for o, a in enumerate((1, 0)):
                    for g in range(G4):
                        if not isinstance(i, int):
                            sp.wait_ge(stats_read, 8 * i - 8 + G4 * o + g + 1)
                        sp.dma_start(xb[:, a, g, :], x_v[even + a, g % 2, g // 2])\
                          .then_inc(x_in[a][g], 16)

            stat_loads(0, NI - 2)
            with sp.Fori(1, NI // 2) as i:
                stat_loads(i, i * -2 + (NI - 2))

            def crow_load(m):
                sp.wait_ge(cs8_ready, m + 1)
                at_least(sp, hsum_ready, m)
                for k in range(2 * SCH):
                    sp.dma_start(crow[SROWS * k:SROWS * (k + 1), 1:W + 1],
                                 cs8[k:k + 1, :].rearrange("a (r w) -> a r w", w=W)).then_inc(crow_in, 16)

            def store(n, a, g):
                sp.wait_ge(added, 4 * n + g + 1)
                sp.dma_start(out_v[n, g % 2, g // 2], xb[:, a, g, :]).then_inc(x_out[a][g], 16)

            def load(n, a, g, pair, ahead):
                src = x_v[n] if pair is None else x_pairs[pair + ahead // 2, ahead % 2]
                sp.wait_ge(x_out[a][g], 8 * (n - a))
                sp.dma_start(xb[:, a, g, :], src[g % 2, g // 2]).then_inc(x_in[a][g], 16)

            def image(n, a, loads, last_loads, prep, first=False, pair=None):
                sp.wait_ge(bm_ready, n + 1)
                sp.dma_start(map_rows[n].rearrange("(h i r j) -> h r i j", h=2, i=4, r=HR)[0],
                             bm[0:HR]).then_inc(bm_stored, 16)
                sp.dma_start(map_rows[n].rearrange("(h i r j) -> h r i j", h=2, i=4, r=HR)[1],
                             bm[HR:H]).then_inc(bm_stored, 16)
                sp.wait_ge(bm_stored, 32 * n + 32)
                for h in range(2):
                    if not first:
                        sp.wait_ge(scaled, 4 * n - 2 + 2 * h)
                    sp.dma_start(bmap[:, h, :],
                                 map_rows[bass.ds(n, 1), h * HPX:(h + 1) * HPX].to_broadcast([P, HPX]))\
                      .then_inc(bmap_in[h], 16)
                if not first:
                    store(n - 1, 1 - a, 3)
                    if last_loads:
                        load(n + 1, 1 - a, 3, pair, 2 - a)
                for g in range(3):
                    if prep and g == 2:
                        crow_load(n + 1)
                    store(n, a, g)
                    if loads:
                        load(n + 2, a, g, pair, 3 - a)

            crow_load(0)
            image(0, 0, loads=True, last_loads=False, prep=True, first=True)
            with sp.Fori(0, (NI - 4) // 2) as i:
                image(2 * i + 1, 1, loads=True, last_loads=True, prep=True, pair=i)
                image(2 * i + 2, 0, loads=True, last_loads=True, prep=True, pair=i)
            image(NI - 3, 1, loads=True, last_loads=True, prep=True)
            image(NI - 2, 0, loads=False, last_loads=True, prep=True)
            image(NI - 1, 1, loads=False, last_loads=False, prep=False)
            store(NI - 1, 1, 3)
            for a in range(2):
                for g in range(G4):
                    sp.wait_ge(x_out[a][g], 16 * (NI // 2))

        @block.gpsimd
        def _(pool):
            done = [0]

            def after_own():
                pool.wait_ge(w_pool, done[0])

            def signal(ins):
                ins.then_inc(w_pool, 1)
                done[0] += 1

            pool.wait_ge(wmax, 1)
            nc.gpsimd.partition_all_reduce(mxb[:, :], scl[:, :], P, bass.bass_isa.ReduceOp.max)\
              .then_inc(wall, 1)
            pool.wait_ge(wscale, 1)
            for ci in range(CT):
                w0, w1, w2 = (wt[:, ci, :, d, :] for d in range(3))
                E, PP, Q, G0, G2, HH = (wtmp[:, k] for k in range(6))
                for dy in range(3):
                    signal(nc.gpsimd.tensor_tensor(
                        wt[:, ci, dy], wt[:, ci, dy], scl[:, None, :].to_broadcast([P, 3, C]), ALU.mult))
                if ci:
                    pool.wait_ge(w_act, WA * ci)
                after_own()
                signal(nc.gpsimd.tensor_tensor(E, w0, w2, ALU.add))
                after_own()
                signal(nc.gpsimd.tensor_tensor(PP, E, w1, ALU.add))
                signal(nc.gpsimd.tensor_tensor(Q, E, w1, ALU.subtract))
                pool.wait_ge(w_act, WA * ci + 3)
                signal(nc.gpsimd.tensor_tensor(G0, G0, G2, ALU.add))
                after_own()
                signal(nc.gpsimd.tensor_tensor(G2, G0, HH, ALU.add))
                signal(nc.gpsimd.tensor_tensor(HH, G0, HH, ALU.subtract))
                for o, (k, src) in enumerate(((0, w0), (5, w2), (1, PP), (2, Q), (3, G2), (4, HH))):
                    pool.wait_ge(w_act, WA * ci + 6 + o + 1)
                    signal(nc.gpsimd.tensor_tensor(U[:, ci, 1, k], src, U[:, ci, 0, k], ALU.subtract))
            after_own()
            for a in range(2):
                for ci in range(CT):
                    for e in (0, (H + 1) * J):
                        last = nc.gpsimd.memset(V[:, a, ci, :, e:e + J], 0.0)
                        last.then_inc(weights_ready, 1)

            def add_x(n, a, g):
                pool.wait_ge(scaled, 4 * n + g + 1)
                xv = xb[:, a, g, :].rearrange("p (r j i) -> p r j i", j=J, i=4)
                yv = y[:, g % 2].rearrange("p i (r j) -> p r j i", j=J)
                nc.gpsimd.tensor_tensor(xv, xv, yv, ALU.add).then_inc(added, 1)

            def sum_rest(m, h):
                pool.wait_ge(hi_ready, 2 * m + h + 1)
                nc.gpsimd.tensor_tensor(slo[:, :], ssum[:, :], shi[:, :], ALU.subtract).then_inc(lo_ready, 1)

            def image(n, a, prep=True, first=False):
                if not first:
                    add_x(n - 1, 1 - a, 3)
                add_x(n, a, 0)
                if prep:
                    sum_rest(n + 1, 0)
                add_x(n, a, 1)
                if prep:
                    sum_rest(n + 1, 1)
                add_x(n, a, 2)

            sum_rest(0, 0)
            sum_rest(0, 1)
            image(0, 0, first=True)
            with pool.Fori(0, (NI - 2) // 2) as i:
                image(2 * i + 1, 1)
                image(2 * i + 2, 0)
            image(NI - 1, 1, prep=False)
            add_x(NI - 1, 1, 3)

        @block.scalar
        def _(act):
            for c in range(CT):
                act.dma_start(wt[:, c], w_v[:, c].rearrange("p (a b o) -> p a b o", a=3, b=3)).then_inc(w_in, 16)
            act.dma_start(cst[:, :], consts).then_inc(cst_in, 16)
            for k, v in enumerate((gamma, beta, conv_b)):
                act.dma_start(vec[:, k, :], v).then_inc(vec_in, 16)
            act.dma_start(bb[:, :], beta_b.to_broadcast([P, 1])).then_inc(vec_in, 16)

            for ci in range(CT):
                w0, w1, w2 = (wt[:, ci, :, d, :] for d in range(3))
                E, PP, Q, G0, G2, HH = (wtmp[:, k] for k in range(6))
                base = WP * ci
                act.wait_ge(w_pool, base + 3)
                nc.scalar.activation(G0, w0, ACT.Copy, scale=1 / 24).then_inc(w_act, 1)
                nc.scalar.activation(G2, w2, ACT.Copy, scale=1 / 6).then_inc(w_act, 1)
                nc.scalar.activation(HH, w1, ACT.Copy, scale=1 / 12).then_inc(w_act, 1)
                act.wait_ge(w_pool, base + 6)
                act.wait_ge(w_act, WA * ci + 3)
                nc.scalar.activation(w0, w0, ACT.Copy, scale=1 / 4).then_inc(w_act, 1)
                nc.scalar.activation(PP, PP, ACT.Copy, scale=-1 / 6).then_inc(w_act, 1)
                nc.scalar.activation(Q, Q, ACT.Copy, scale=-1 / 6).then_inc(w_act, 1)
                act.wait_ge(w_act, WA * ci + 6)
                act.wait_ge(w_pool, base + 9)
                for k, src in ((0, w0), (5, w2), (1, PP), (2, Q), (3, G2), (4, HH)):
                    nc.scalar.activation(U[:, ci, 0, k], src, ACT.Copy).then_inc(w_act, 1)

            for k, (n_in, src) in enumerate(((NI * CT, tmp[:, 2, :]), (CT, bnv[:, 2, :]))):
                act.wait_ge(root_in, k + 1)
                dst = tmp[:, 3, :] if k == 0 else bnv[:, 3, :]
                nc.scalar.activation(dst, src, ACT.Sqrt).then_inc(root_out, 1)

            def coefficients(m, a):
                src = AB[:, m:m + 1] if isinstance(m, int) else AB[:, bass.ds(m, 1)]
                nc.scalar.activation(ab[:, a:a + 1], src, ACT.Copy).then_inc(ab_ready, 1)
                act.wait_ge(ab_ready, m + 1)

            def signs(m, a, g):
                s = 4 * m + g
                c = g % 2
                act.wait_ge(x_in[a][g], arrived(m, a))
                at_least(act, t_ready, 3 * s)
                nc.scalar.activation(u[:, :, 1:W + 1], xb[:, a, g, :].rearrange("p (r w) -> p r w", w=W),
                                     ACT.Sign, scale=ab[:, a, 0, c:c + 1], bias=ab[:, a, 1, c:c + 1])\
                  .then_inc(u_ready, 1)
                at_least(act, v_ready, s)
                act.wait_ge(u_ready, s + 1)
                col = lambda first, step, count: u[:, :, first:first + 4 * J].rearrange(
                    "p r (j q) -> p q r j", q=4)[:, 0:(count - 1) * step + 1:step]
                view = lambda t: t.rearrange("p q (r j) -> p q r j", j=J)
                nc.scalar.activation(view(T[:, 0:4]), col(2, 1, 4), ACT.Relu, scale=2.0).then_inc(t_ready, 1)
                nc.scalar.activation(view(T4[:, :]), col(0, 1, 4), ACT.Relu, scale=8.0).then_inc(t_ready, 1)
                nc.scalar.activation(view(T[:, 4:6]), col(1, 2, 2), ACT.Relu, scale=4.0).then_inc(t_ready, 1)

            def absolute(m, a, g):
                c, h = g % 2, g // 2
                act.wait_ge(x_in[a][g], arrived(m, a))
                at_least(act, s_ready, 2 * m + h)
                nc.scalar.activation(r[:, c, :], xb[:, a, g, :], ACT.Abs, scale=ab[:, a, 0, c:c + 1],
                                     bias=ab[:, a, 1, c:c + 1]).then_inc(abs_done, 1)
                if c == 1:
                    act.wait_ge(abs_done, 4 * m + g + 1)
                    nc.scalar.activation(r[:, c, :], r[:, c, :], ACT.Relu, scale=-1.0, bias=1.0)\
                      .then_inc(q_ready, 1)

            def sum_high(m, h):
                act.wait_ge(s_ready, 2 * m + h + 1)
                at_least(act, cs_done, 2 * m + h)
                nc.scalar.activation(shi[:, :], ssum[:, :], ACT.Copy).then_inc(hi_ready, 1)

            def channel_sums(m):
                act.wait_ge(cs_done, 2 * m + 2)
                at_least(act, crow_in, 128 * m)
                nc.scalar.activation(cs8[:, :], csum[0:2 * SCH, 0:SN], ACT.Copy, bias=float(P))\
                  .then_inc(cs8_ready, 1)

            def evacuate(n, g):
                act.wait_ge(m13_done, 4 * n + g + 1)
                at_least(act, sd_done, 2 * (4 * n + g))
                nc.scalar.activation(m13[:, :, :], acc[:, 0:2, 0:N], ACT.Copy,
                                     scale=inv_s[:, g % 2:g % 2 + 1]).then_inc(ev13, 1)

            act.wait_ge(coef_ready, 1)
            act.wait_ge(pads, 4)
            coefficients(0, 0)
            for h in range(2):
                for g in (2 * h, 2 * h + 1):
                    absolute(0, 0, g)
                    signs(0, 0, g)
                sum_high(0, h)
            channel_sums(0)

            def image(n, a, prep=True):
                if prep:
                    coefficients(n + 1, 1 - a)
                for g in range(G4):
                    if prep and g == 3:
                        sum_high(n + 1, 1)
                    if prep:
                        signs(n + 1, 1 - a, g)
                    evacuate(n, g)
                    if prep and g == 1:
                        sum_high(n + 1, 0)
                    if prep:
                        for k in ((0, 1), (2,), (3,), ())[g]:
                            absolute(n + 1, 1 - a, k)
                        if g == 3:
                            channel_sums(n + 1)

            act.wait_ge(scale_ready, 2)
            image(0, 0)
            with act.Fori(0, (NI - 2) // 2) as i:
                image(2 * i + 1, 1)
                image(2 * i + 2, 0)
            image(NI - 1, 1, prep=False)

        @block.tensor
        def _(pe):
            pe.wait_ge(wrow, 1)
            for c in range(CT):
                last = nc.tensor.matmul(box[:, c:c + 1], mxb[0:1, c * P:(c + 1) * P], one[:, :],
                                        start=True, stop=True)
            last.then_inc(scale_ready, 1)
            pe.wait_ge(cst_in, 16)
            grouped = cst[:, C_GROUP:C_GROUP + P]
            pe.wait_ge(mv_done, NI // 2)
            nc.tensor.matmul(csum[:, 0:NI * CT], grouped, mv[:, :, :, 0].rearrange("p n c -> p (n c)"),
                             start=True, stop=True).then_inc(grp, 1)
            pe.wait_ge(mean_ready, 1)
            nc.tensor.matmul(acc[:, 0, 0:NI * CT], grouped, tmp[:, 1, :], start=True, stop=True)\
              .then_inc(grp, 1)

            def sums(m, h):
                pe.wait_ge(hi_ready, 2 * m + h + 1)
                pe.wait_ge(lo_ready, 2 * m + h + 1)
                if h == 0:
                    at_least(pe, cs8_ready, m)
                    if isinstance(m, int) and m == 0:
                        pe.wait_ge(coef_ready, 1)
                for k in range(SCH):
                    j = SCH * h + k
                    for part in (shi, slo):
                        last = nc.tensor.matmul(
                            csum[0:2 * SCH, 0:SN], sel[:, 7 - j:15 - j], part[:, k * SN:(k + 1) * SN],
                            start=(j == 0 and part is shi), stop=(j == 2 * SCH - 1 and part is slo))
                last.then_inc(cs_done, 1)

            def boxed(n):
                pe.wait_ge(hsum_ready, n + 1)
                at_least(pe, bm_ready, n)
                nc.tensor.matmul(box[:, 0:W], cst[0:H, C_TRI:C_TRI + P], hsum[:, 1, :],
                                 start=True, stop=True).then_inc(box_done, 1)

            def products(n, a, g, pair):
                h, co = g // 2, g % 2
                free, count = ((ev13, 1), (sd_done, 2), (y05_done, 1))[pair]
                at_least(pe, free, count * (4 * n + g))
                for b in (2 * pair, 2 * pair + 1):
                    k = BANKS[b]
                    for ci in range(CT):
                        for dy in range(3):
                            at = (HR * h + dy) * J
                            for part in range(2):
                                last = nc.tensor.matmul(
                                    acc[:, b, 0:N], U[:, ci, part, k, dy, co * P:(co + 1) * P],
                                    V[:, a, ci, VPLANE[k], at:at + N],
                                    start=(ci + dy + part == 0), stop=(ci == CT - 1 and dy == 2 and part == 1))
                last.then_inc((m13_done, m24_done, m05_done)[pair], 1)

            def image(n, a, prep=True):
                pe.wait_ge(v_ready, 4 * n + 4)
                for g in range(G4):
                    products(n, a, g, 0)
                    if g == 0:
                        boxed(n)
                    if prep and g == 2:
                        sums(n + 1, 0)
                    products(n, a, g, 1)
                    if prep and g == 3:
                        sums(n + 1, 1)
                    products(n, a, g, 2)

            sums(0, 0)
            sums(0, 1)
            pe.wait_ge(weights_ready, 2 * 2 * CT)
            image(0, 0)
            with pe.Fori(0, (NI - 2) // 2) as i:
                image(2 * i + 1, 1)
                image(2 * i + 2, 0)
            image(NI - 1, 1, prep=False)

        @block.vector
        def _(dve):
            steps = [0]

            def chain(ins):
                steps[0] += 1
                ins.then_inc(step, 1)
                dve.wait_ge(step, steps[0])

            nc.vector.memset(one[:, :], 1.0).then_inc(pads, 1)
            nc.vector.memset(u[:, :, :], 0.5).then_inc(pads, 1)
            nc.vector.memset(crow[:, :], 0.0).then_inc(pads, 1)
            dve.wait_ge(w_in, 16 * CT)
            for c in range(CT):
                chain(nc.vector.tensor_reduce((scl, mxb)[c][:, :], wt[:, c].rearrange("p a b o -> p o (a b)"),
                                              AX.X, ALU.max, apply_absolute_value=True))
            nc.vector.tensor_tensor(scl[:, :], scl[:, :], mxb[:, :], ALU.max).then_inc(wmax, 1)

            def statistics(i):
                for o, a in enumerate((1, 0)):
                    for g in range(G4):
                        c, h = g % 2, g // 2
                        dve.wait_ge(x_in[a][g], 16 * i + 16)
                        for k in range(4):
                            last = nc.vector.bn_stats(st[:, a, c, 4 * h + k], xb[:, a, g, k * N:(k + 1) * N])
                        last.then_inc(stats_read, 1)
                    for c in range(CT):
                        dve.wait_ge(stats_read, 8 * i + G4 * o + 3 + c)
                        nc.vector.memset(mark[:, a, c:c + 1], 0.0)
                        nc.vector.bn_aggr(mvt[:, a, c, :], st[:, a, c]).then_inc(aggr_done, 1)
                dve.wait_ge(aggr_done, 4 * i + 4)
                nc.vector.tensor_copy(mv[:, bass.ds(NI - 2 - 2 * i, 2)], mvt[:, :]).then_inc(mv_done, 1)

            statistics(0)
            dve.wait_ge(wall, 1)
            chain(nc.vector.tensor_scalar(mxb[:, :], mxb[:, :], 1e-30, None, ALU.max))
            chain(nc.vector.tensor_scalar(mxb[:, :].bitcast(U32), mxb[:, :].bitcast(U32), 0x7F800000, None,
                                          ALU.bitwise_and))
            chain(nc.vector.reciprocal(scl[:, :], mxb[:, :]))
            chain(nc.vector.tensor_scalar(scl[:, :], scl[:, :], 2.0 ** 14, None, ALU.mult))
            nc.vector.tensor_scalar(mxb[:, :], mxb[:, :], 2.0 ** -14, None, ALU.mult).then_inc(wrow, 1)
            nc.vector.memset(crow[:, 0:1], 0.0).then_inc(wscale, 1)
            dve.wait_ge(scale_ready, 1)
            chain(nc.vector.tensor_copy(inv_s[:, :], box[:, 0:CT]))
            nc.vector.tensor_scalar(neg_inv[:, :], inv_s[:, :], -1.0, None, ALU.mult).then_inc(scale_ready, 1)
            dve.wait_ge(cst_in, 16)
            dve.wait_ge(vec_in, 64)
            nc.vector.tensor_copy(sel[:, :], cst[:, C_SEL:C_SEL + 15]).then_inc(pads, 1)
            chain(nc.vector.tensor_scalar(rcount[:, :], cst[0:H, C_COUNT:C_COUNT + W], float(C), bb[0:H, :],
                                          ALU.mult, ALU.add))
            chain(nc.vector.reciprocal(rcount[:, :], rcount[:, :]))
            with dve.Fori(1, NI // 2) as i:
                statistics(i)

            mean = mv[:, :, :, 0].rearrange("p n c -> p (n c)")
            var = mv[:, :, :, 1].rearrange("p n c -> p (n c)")
            d, t1, gv, a_ = (tmp[:, k, :] for k in range(4))
            t4, t5, mg = (tmp[:, k, :] for k in range(4, 7))
            by_c = lambda t: t.rearrange("p (n c) -> p c n", c=CT)
            dve.wait_ge(mv_done, NI // 2)
            dve.wait_ge(grp, 1)
            chain(nc.vector.tensor_copy(mg, csum[:, 0:NI * CT]))
            chain(nc.vector.tensor_tensor(d, mean, mg, ALU.subtract))
            chain(nc.vector.tensor_tensor(t1, d, d, ALU.mult))
            nc.vector.tensor_tensor(t1, t1, var, ALU.add).then_inc(mean_ready, 1)
            dve.wait_ge(grp, 2)
            nc.vector.tensor_scalar(gv, acc[:, 0, 0:NI * CT], GN_EPS, None, ALU.add).then_inc(root_in, 1)

            def inverse_root(v, s, t):
                chain(nc.vector.reciprocal(s, s))
                chain(nc.vector.tensor_tensor(t, s, s, ALU.mult))
                chain(nc.vector.tensor_tensor(t, t, v, ALU.mult))
                chain(nc.vector.tensor_scalar(t, t, -0.5, 1.5, ALU.mult, ALU.add))
                chain(nc.vector.tensor_tensor(s, s, t, ALU.mult))

            dve.wait_ge(root_out, 1)
            inverse_root(gv, a_, t4)
            mu, vs, bv, rs, bt, off = (bnv[:, k, :] for k in range(6))
            chain(nc.vector.tensor_tensor(t5, a_, d, ALU.mult))
            chain(nc.vector.tensor_reduce(mu, by_c(t5), AX.X, ALU.add))
            chain(nc.vector.tensor_scalar(mu, mu, 1.0 / NI, None, ALU.mult))
            for c in range(CT):
                chain(nc.vector.tensor_scalar(by_c(t1)[:, c], by_c(t5)[:, c], mu[:, c:c + 1], None,
                                              ALU.subtract))
            chain(nc.vector.tensor_tensor(t1, t1, t1, ALU.mult))
            chain(nc.vector.tensor_tensor(t4, a_, a_, ALU.mult))
            chain(nc.vector.tensor_tensor(t4, t4, var, ALU.mult))
            chain(nc.vector.tensor_tensor(t4, t4, t1, ALU.add))
            chain(nc.vector.tensor_reduce(vs, by_c(t4), AX.X, ALU.add))
            nc.vector.tensor_scalar(bv, vs, 1.0 / NI, BN_EPS, ALU.mult, ALU.add).then_inc(root_in, 1)
            dve.wait_ge(root_out, 2)
            inverse_root(bv, rs, bt)
            chain(nc.vector.tensor_tensor(rs, rs, vec[:, 0, :], ALU.mult))
            chain(nc.vector.tensor_tensor(off, rs, mu, ALU.mult))
            chain(nc.vector.tensor_tensor(off, vec[:, 1, :], off, ALU.subtract))
            for c in range(CT):
                chain(nc.vector.tensor_scalar(AB[:, :, 0, c], by_c(a_)[:, c], rs[:, c:c + 1], None, ALU.mult))
                chain(nc.vector.tensor_tensor(AB[:, :, 2, c], AB[:, :, 0, c], by_c(mg)[:, c], ALU.mult))
                chain(nc.vector.tensor_scalar(AB[:, :, 2, c], AB[:, :, 2, c], off[:, c:c + 1], None,
                                              ALU.subtract))
                chain(nc.vector.tensor_scalar(AB[:, :, 1, c], AB[:, :, 2, c], -1.0, None, ALU.mult))
            nc.vector.memset(mvt[:, :, :, :], 0.0).then_inc(coef_ready, 1)

            def transform(m, a, g):
                c, h = g % 2, g // 2
                s = 4 * m + g
                at = (1 + HR * h) * J
                vk = lambda k, n=1: V[:, a, c, VPLANE[k]:VPLANE[k] + n, at:at + N]
                if not (isinstance(m, int) and m == 0):
                    dve.wait_ge(m05_done, 4 * m - 4)
                dve.wait_ge(t_ready, 3 * s + 2)
                nc.vector.tensor_tensor(cq[:, :, :], T[:, 0:4], T4[:, :], ALU.subtract).then_inc(cq_done, 1)
                dve.wait_ge(t_ready, 3 * s + 3)
                nc.vector.tensor_tensor(aq[:, :, :], T[:, 2:6:3], T[:, 0:5:4], ALU.subtract).then_inc(aq_done, 1)
                dve.wait_ge(cq_done, s + 1)
                nc.vector.tensor_tensor(vk(0, 2), cq[:, 2:4], cq[:, 0:2], ALU.subtract)
                nc.vector.scalar_tensor_tensor(out=vk(1), in0=cq[:, 2:3], scalar=6.0, in1=cq[:, 1:2],
                                               op0=ALU.add, op1=ALU.add)
                nc.vector.tensor_tensor(vk(2), cq[:, 2:3], cq[:, 1:2], ALU.subtract)
                dve.wait_ge(aq_done, s + 1)
                nc.vector.tensor_tensor(vk(3), aq[:, 0:1], aq[:, 1:2], ALU.add)
                nc.vector.tensor_tensor(vk(4), aq[:, 0:1], aq[:, 1:2], ALU.subtract).then_inc(v_ready, 1)

            def pair_sum(m, h):
                dve.wait_ge(abs_done, 4 * m + 2 * h + 1)
                dve.wait_ge(q_ready, 2 * m + h + 1)
                at_least(dve, lo_ready, 2 * m + h)
                nc.vector.scalar_tensor_tensor(out=ssum[:, :], in0=r[:, 0, :], scalar=1.0, in1=r[:, 1, :],
                                               op0=ALU.min, op1=ALU.subtract).then_inc(s_ready, 1)

            def columns(n):
                dve.wait_ge(crow_in, 128 * n + 128)
                nc.vector.tensor_tensor(hsum[:, 0, :], crow[:, 0:W], crow[:, 1:W + 1], ALU.add)\
                  .then_inc(hpart, 1)
                dve.wait_ge(hpart, n + 1)
                at_least(dve, box_done, n)
                nc.vector.tensor_tensor(hsum[:, 1, :], hsum[:, 0, :], crow[:, 2:W + 2], ALU.add)\
                  .then_inc(hsum_ready, 1)

            def beta_map(n):
                dve.wait_ge(box_done, n + 1)
                at_least(dve, bm_stored, 32 * n)
                nc.vector.scalar_tensor_tensor(
                    out=bm[:, :, :].rearrange("p i j -> p j i"),
                    in0=box[0:H, 0:W].rearrange("p (j i) -> p j i", i=4), scalar=bb[0:H, :],
                    in1=rcount[:, :].rearrange("p (j i) -> p j i", i=4), op0=ALU.add, op1=ALU.mult)\
                  .then_inc(bm_ready, 1)

            def sums_and_differences(n, g):
                co = g % 2
                dve.wait_ge(m24_done, 4 * n + g + 1)
                dve.wait_ge(ev13, 4 * n + g + 1)
                for k, scale in ((0, inv_s), (2, neg_inv)):
                    nc.vector.scalar_tensor_tensor(
                        out=sd[:, k:k + 2], in0=acc[:, 2:4, 0:N], scalar=scale[:, co:co + 1], in1=m13[:, :],
                        op0=ALU.mult, op1=ALU.add).then_inc(sd_done, 1)

            def finish(n, g):
                co, h = g % 2, g // 2
                s = 4 * n + g
                yb = y[:, g % 2]
                dve.wait_ge(m05_done, s + 1)
                dve.wait_ge(sd_done, 2 * s + 2)
                if not isinstance(n, int) or s >= 2:
                    dve.wait_ge(added, s - 1)
                nc.vector.scalar_tensor_tensor(
                    out=yb[:, 0:4:3], in0=acc[:, 4:6, 0:N], scalar=inv_s[:, co:co + 1], in1=sd[:, 0:4:2],
                    op0=ALU.mult, op1=ALU.add).then_inc(y05_done, 1)
                nc.vector.scalar_tensor_tensor(out=yb[:, 1], in0=sd[:, 3], scalar=2.0, in1=sd[:, 2],
                                               op0=ALU.mult, op1=ALU.add)
                nc.vector.scalar_tensor_tensor(out=yb[:, 2], in0=sd[:, 1], scalar=4.0, in1=sd[:, 0],
                                               op0=ALU.mult, op1=ALU.add)
                dve.wait_ge(y05_done, s + 1)
                nc.vector.tensor_tensor(yb[:, 0], yb[:, 0], sd[:, 1], ALU.add)
                nc.vector.scalar_tensor_tensor(out=yb[:, 3], in0=sd[:, 3], scalar=8.0, in1=yb[:, 3],
                                               op0=ALU.mult, op1=ALU.add).then_inc(y_done, 1)
                dve.wait_ge(y_done, s + 1)
                dve.wait_ge(bmap_in[h], 16 * n + 16)
                flat = yb.rearrange("p i n -> p (i n)")
                nc.vector.scalar_tensor_tensor(out=flat, in0=flat, scalar=vec[:, 2, co:co + 1], in1=bmap[:, h, :],
                                               op0=ALU.add, op1=ALU.mult).then_inc(scaled, 1)

            dve.wait_ge(weights_ready, 2 * 2 * CT)
            for g in range(G4):
                transform(0, 0, g)
                if g % 2:
                    pair_sum(0, g // 2)

            def image(n, a, prep=True, first=False):
                for g in range(G4):
                    if g == 0:
                        columns(n)
                    if prep and g == 1:
                        pair_sum(n + 1, 0)
                    if g > 0:
                        finish(n, g - 1)
                    elif not first:
                        finish(n - 1, 3)
                    if g == 0:
                        beta_map(n)
                    if prep:
                        transform(n + 1, 1 - a, g)
                    sums_and_differences(n, g)
                    if prep and g == 2:
                        pair_sum(n + 1, 1)

            image(0, 0, first=True)
            with dve.Fori(0, (NI - 2) // 2) as i:
                image(2 * i + 1, 1)
                image(2 * i + 2, 0)
            image(NI - 1, 1, prep=False)
            finish(NI - 1, 3)


def kernel(x, L0_conv_bn_gamma, L0_conv_bn_beta, L0_conv_conv_w, L0_conv_conv_b, L0_conv_beta_conv_b):
    import numpy as np
    import concourse.bacc as bacc
    from concourse.bass_utils import run_bass_kernel_spmd

    def column(v):
        return np.ascontiguousarray(np.asarray(v).reshape(CT, P).T)

    k = np.arange(P)
    group = (k[:, None] // GROUP == k[None, :] // GROUP).astype(np.float32) / GROUP
    consts = np.zeros((P, C_WIDTH), np.float32)
    consts[:, C_GROUP:C_GROUP + P] = group
    consts[:, C_SEL + 7] = 1.0
    rows = np.arange(H)
    consts[:H, C_TRI:C_TRI + H] = abs(rows[:, None] - rows[None, :]) <= 1
    near = 3.0 - (rows == 0) - (rows == H - 1)
    consts[:H, C_COUNT:C_COUNT + W] = near[:, None] * near[None, :]

    w = np.asarray(L0_conv_conv_w)
    arrays = {
        "x": np.ascontiguousarray(x),
        "w_t": np.ascontiguousarray(w.transpose(1, 2, 3, 0)).reshape(C, 9, C),
        "gamma": column(L0_conv_bn_gamma),
        "beta": column(L0_conv_bn_beta),
        "conv_b": column(L0_conv_conv_b),
        "beta_b": np.asarray(L0_conv_beta_conv_b).reshape(1, 1),
        "consts": consts,
    }
    nc = bacc.Bacc("TRN2", target_bir_lowering=False, num_devices=1)
    args = {name: nc.dram_tensor(name, v.shape, F32, kind="ExternalInput").ap() for name, v in arrays.items()}
    map_rows = nc.dram_tensor("map_rows", (NI, H * W), F32, kind="Internal").ap()
    out = nc.dram_tensor("out", (NI, C, H, W), F32, kind="ExternalOutput").ap()
    conv_preact(nc, args["x"], args["w_t"], args["gamma"], args["beta"], args["conv_b"], args["beta_b"],
                args["consts"], map_rows, out)
    r = run_bass_kernel_spmd(nc, [arrays], core_ids=[0])
    return r.results[0]["out"]
```

```python
from contextlib import ExitStack

import concourse.bass as bass
from concourse import mybir

F32 = mybir.dt.float32
F16 = mybir.dt.float16
U32 = mybir.dt.uint32
ALU = mybir.AluOpType
ACT = mybir.ActivationFunctionType
AX = mybir.AxisListType

P = 128
NI, C, H, W = 16, 256, 56, 56
CT = C // P
HR = H // 2
HPX = HR * W
J = W // 4
N = HR * J
NX = N + J
K6 = 6
G4 = 2 * CT
UP = 60
GROUP = 8
GN_EPS, BN_EPS = 1e-5, 1e-4
SROWS = 7
SN = SROWS * W
SCH = HPX // SN
VPLANE = {0: 0, 5: 1, 1: 2, 2: 3, 3: 4, 4: 5}
BANKS = (1, 3, 2, 4, 0, 5)
C_GROUP, C_SEL, C_TRI, C_COUNT = 0, P, P + 15, P + 15 + P
C_WIDTH = C_COUNT + W
LAST_PARTS = ((G4 * NI - 1, 0, N // 2), (G4 * NI, N // 2, N))


def conv_preact(nc, x, w_t, gamma, beta, conv_b, beta_b, consts, map_rows, out):
    x_v = x.rearrange("n (c p) (h r) w -> n c h p (r w)", p=P, h=2)
    out_v = out.rearrange("n (c p) (h r) w -> n c h p (r w)", p=P, h=2)
    x_pairs = x_v[1:NI - 1].rearrange("(i k) c h p f -> i k c h p f", k=2)
    w_v = w_t.rearrange("(c p) t o -> p c (t o)", p=P)

    with ExitStack() as ctx:
        def sb(name, shape, dt=F32):
            return ctx.enter_context(nc.sbuf_tensor(name, shape, dt))

        def sem(name):
            return ctx.enter_context(nc.semaphore(name))

        xb = sb("xb", [P, 2, CT, 2, HPX])
        U = sb("U", [P, CT, 2, K6, 3, C], F16)
        V = sb("V", [P, 2, CT, K6, (H + 2) * J], F16)
        u = sb("u", [P, HR + 1, UP], F16)
        T = sb("T", [P, K6, NX], F16)
        T4 = sb("T4", [P, 4, NX], F16)
        cq = sb("cq", [P, 4, NX], F16)
        aq = sb("aq", [P, 2, NX], F16)
        r = sb("r", [P, CT, HPX])
        ssum = sb("ssum", [P, HPX])
        shi = sb("shi", [P, HPX], F16)
        slo = sb("slo", [P, HPX], F16)
        sel = sb("sel", [P, 15], F16)
        bmap = sb("bmap", [P, 2, HPX])
        m13 = sb("m13", [P, 2, N])
        sd = sb("sd", [P, 4, N])
        y = sb("y", [P, 2, 4, N])
        cs8 = sb("cs8", [2 * SCH, SN])
        crow = sb("crow", [H, W + 2])
        hsum = sb("hsum", [H, 2, W])
        bm = sb("bm", [H, 4, J])
        rcount = sb("rcount", [H, W])
        cst = sb("cst", [P, C_WIDTH])
        vec = sb("vec", [P, 3, CT])
        bb = sb("bb", [P, 1])
        one = sb("one", [1, 1])
        mxb = sb("mxb", [P, C])
        scl = sb("scl", [P, C])
        inv_s = sb("inv_s", [P, CT])
        neg_inv = sb("neg_inv", [P, CT])
        st = sb("st", [P, 2, CT, 8, 6])
        mark = sb("mark", [P, 2, CT])
        mvt = sb("mvt", [P, 2, CT, 2])
        mv = sb("mv", [P, NI, CT, 2])
        tmp = sb("tmp", [P, 8, NI * CT])
        bnv = sb("bnv", [P, 8, CT])
        AB = sb("AB", [P, NI, 2, CT])
        eps = sb("eps", [P, 2])
        ab = sb("ab", [P, 2, 2, CT])
        scratch = V[:, :, :, :, :].rearrange("p a c k n -> p (a c k n)").bitcast(F32)
        wt = scratch[:, 0:CT * 9 * C].rearrange("p (c a b o) -> p c a b o", c=CT, a=3, b=3)
        wtmp = scratch[:, CT * 9 * C:CT * 9 * C + 6 * 3 * C].rearrange("p (k a o) -> p k a o", k=6, a=3)

        acc = ctx.enter_context(nc.psum_tensor("acc", [P, K6, 512], F32))
        csum = ctx.enter_context(nc.psum_tensor("csum", [P, 512], F32))
        box = ctx.enter_context(nc.psum_tensor("box", [P, 512], F32))

        w_in = [sem(f"w_in{c}") for c in range(CT)]
        vec_in, cst_in = sem("vec_in"), sem("cst_in")
        x_in = [[sem(f"x_in{a}{g}") for g in range(G4)] for a in range(2)]
        x_out = [[sem(f"x_out{a}{g}") for g in range(G4)] for a in range(2)]
        stats_read, aggr_done, mv_done = sem("stats_read"), sem("aggr_done"), sem("mv_done")
        wmax, wall, wrow, wscale = sem("wmax"), sem("wall"), sem("wrow"), sem("wscale")
        w_pool, w_act, scale_ready = sem("w_pool"), sem("w_act"), sem("scale_ready")
        step, dev_ready, grp = sem("step"), sem("dev_ready"), sem("grp")
        var_ready, root_out, coef_ready = (
            sem(s) for s in ("var_ready", "root_out", "coef_ready"))
        pads, weights_ready = sem("pads"), sem("weights_ready")
        ab_ready, u_ready, t_ready, cq_done, aq_done, v_ready = (
            sem(s) for s in ("ab_ready", "u_ready", "t_ready", "cq_done", "aq_done", "v_ready"))
        hi_ready, lo_ready = sem("hi_ready"), sem("lo_ready")
        clip, abs_done, q_ready, s_ready, cs_done, cs8_ready, crow_in = (
            sem(s) for s in ("clip", "abs_done", "q_ready", "s_ready", "cs_done", "cs8_ready", "crow_in"))
        hpart, hsum_ready, box_done, bm_ready, bm_stored = (
            sem(s) for s in ("hpart", "hsum_ready", "box_done", "bm_ready", "bm_stored"))
        bmap_in = [sem(f"bmap_in{h}") for h in range(2)]
        last_added = sem("last_added")
        m13_done, m24_done, m05_done, ev13, sd_done, y05_done, y_done, scaled, added = (
            sem(s) for s in ("m13_done", "m24_done", "m05_done", "ev13", "sd_done", "y05_done",
                             "y_done", "scaled", "added"))

        WA = 12
        WP = 15
        STAT_LOADS = 16 * (NI // 2)

        def arrived(n, parity):
            return STAT_LOADS + 8 * (n - parity)

        def at_least(eng, s, value):
            if not (isinstance(value, int) and value <= 0):
                eng.wait_ge(s, value)

        def chunk(a, g):
            return xb[:, a, g % 2, g // 2, :]

        def x_and_y(a, g, lo, hi):
            return (chunk(a, g)[:, 4 * lo:4 * hi].rearrange("p (r j i) -> p r j i", j=J, i=4),
                    y[:, g % 2, :, lo:hi].rearrange("p i (r j) -> p r j i", j=J))

        def rows_of(m, g):
            halo = isinstance(m, int) and m == 0
            return (HR * (g // 2) + halo * (g // 2), HR + (-halo if g // 2 else halo))

        block = ctx.enter_context(nc.Block())

        @block.sync
        def _(sp):
            def stat_loads(i, even):
                for o, a in enumerate((1, 0)):
                    for g in range(G4):
                        if not isinstance(i, int):
                            sp.wait_ge(stats_read, 8 * i - 8 + G4 * o + g + 1)
                        sp.dma_start(chunk(a, g), x_v[even + a, g % 2, g // 2])\
                          .then_inc(x_in[a][g], 16)

            for c in range(CT):
                sp.dma_start(wt[:, c], w_v[:, c].rearrange("p (a b o) -> p a b o", a=3, b=3)).then_inc(w_in[c], 16)
            stat_loads(0, NI - 2)
            with sp.Fori(1, NI // 2) as i:
                stat_loads(i, i * -2 + (NI - 2))

            def crow_load(m):
                sp.wait_ge(cs8_ready, m + 1)
                at_least(sp, hsum_ready, m)
                for k in range(2 * SCH):
                    sp.dma_start(crow[SROWS * k:SROWS * (k + 1), 1:W + 1],
                                 cs8[k:k + 1, :].rearrange("a (r w) -> a r w", w=W)).then_inc(crow_in, 16)

            def store(n, a, g):
                sp.wait_ge(added, 4 * n + g + 1)
                sp.dma_start(out_v[n, g % 2, g // 2], chunk(a, g)).then_inc(x_out[a][g], 16)

            def load(n, a, g, pair, ahead):
                src = x_v[n] if pair is None else x_pairs[pair + ahead // 2, ahead % 2]
                sp.wait_ge(x_out[a][g], 8 * (n - a))
                sp.dma_start(chunk(a, g), src[g % 2, g // 2]).then_inc(x_in[a][g], 16)

            def image(n, a, loads, last_loads, prep, first=False, pair=None):
                sp.wait_ge(bm_ready, n + 1)
                sp.dma_start(map_rows[n].rearrange("(h i r j) -> h r i j", h=2, i=4, r=HR)[0],
                             bm[0:HR]).then_inc(bm_stored, 16)
                sp.dma_start(map_rows[n].rearrange("(h i r j) -> h r i j", h=2, i=4, r=HR)[1],
                             bm[HR:H]).then_inc(bm_stored, 16)
                sp.wait_ge(bm_stored, 32 * n + 32)
                for h in range(2):
                    if not first:
                        sp.wait_ge(scaled, 4 * n - 2 + 2 * h)
                    sp.dma_start(bmap[:, h, :],
                                 map_rows[bass.ds(n, 1), h * HPX:(h + 1) * HPX].to_broadcast([P, HPX]))\
                      .then_inc(bmap_in[h], 16)
                if not first:
                    store(n - 1, 1 - a, 3)
                    if last_loads:
                        load(n + 1, 1 - a, 3, pair, 2 - a)
                for g in range(3):
                    if prep and g == 2:
                        crow_load(n + 1)
                    store(n, a, g)
                    if loads:
                        load(n + 2, a, g, pair, 3 - a)

            crow_load(0)
            image(0, 0, loads=True, last_loads=False, prep=True, first=True)
            with sp.Fori(0, (NI - 4) // 2) as i:
                image(2 * i + 1, 1, loads=True, last_loads=True, prep=True, pair=i)
                image(2 * i + 2, 0, loads=True, last_loads=True, prep=True, pair=i)
            image(NI - 3, 1, loads=True, last_loads=True, prep=True)
            image(NI - 2, 0, loads=False, last_loads=True, prep=True)
            image(NI - 1, 1, loads=False, last_loads=False, prep=False)
            for (s, lo, hi), ready, value in zip(LAST_PARTS, (added, last_added), (G4 * NI, 1)):
                sp.wait_ge(ready, value)
                sp.dma_start(out_v[NI - 1, 1, 1][:, 4 * lo:4 * hi], chunk(1, 3)[:, 4 * lo:4 * hi])\
                  .then_inc(x_out[1][3], 16)
            for a in range(2):
                for g in range(G4):
                    sp.wait_ge(x_out[a][g], 16 * (NI // 2 + (a == 1 and g == 3)))

        @block.gpsimd
        def _(pool):
            done = [0]

            def after_own():
                pool.wait_ge(w_pool, done[0])

            def signal(ins):
                ins.then_inc(w_pool, 1)
                done[0] += 1

            pool.wait_ge(wmax, 1)
            nc.gpsimd.partition_all_reduce(mxb[:, :], scl[:, :], P, bass.bass_isa.ReduceOp.max)\
              .then_inc(wall, 1)
            pool.wait_ge(wscale, 1)
            for ci in range(CT):
                w0, w1, w2 = (wt[:, ci, :, d, :] for d in range(3))
                E, PP, Q, G0, G2, HH = (wtmp[:, k] for k in range(6))
                for dy in range(3):
                    signal(nc.gpsimd.tensor_tensor(
                        wt[:, ci, dy], wt[:, ci, dy], scl[:, None, :].to_broadcast([P, 3, C]), ALU.mult))
                if ci:
                    pool.wait_ge(w_act, WA * ci)
                after_own()
                signal(nc.gpsimd.tensor_tensor(E, w0, w2, ALU.add))
                after_own()
                signal(nc.gpsimd.tensor_tensor(PP, E, w1, ALU.add))
                signal(nc.gpsimd.tensor_tensor(Q, E, w1, ALU.subtract))
                pool.wait_ge(w_act, WA * ci + 3)
                signal(nc.gpsimd.tensor_tensor(G0, G0, G2, ALU.add))
                after_own()
                signal(nc.gpsimd.tensor_tensor(G2, G0, HH, ALU.add))
                signal(nc.gpsimd.tensor_tensor(HH, G0, HH, ALU.subtract))
                for o, (k, src) in enumerate(((0, w0), (5, w2), (1, PP), (2, Q), (3, G2), (4, HH))):
                    pool.wait_ge(w_act, WA * ci + 6 + o + 1)
                    signal(nc.gpsimd.tensor_tensor(U[:, ci, 1, k], src, U[:, ci, 0, k], ALU.subtract))
            after_own()
            for a in range(2):
                for ci in range(CT):
                    for e in (0, (H + 1) * J):
                        last = nc.gpsimd.memset(V[:, a, ci, :, e:e + J], 0.0)
                        last.then_inc(weights_ready, 1)

            def add_x(n, a, g, part=None):
                s, lo, hi = part or (4 * n + g, 0, N)
                pool.wait_ge(scaled, s + 1)
                xv, yv = x_and_y(a, g, lo, hi)
                nc.gpsimd.tensor_tensor(xv, xv, yv, ALU.add).then_inc(added, 1)

            def sum_rest(m, h):
                pool.wait_ge(hi_ready, 2 * m + h + 1)
                nc.gpsimd.tensor_tensor(slo[:, :], ssum[:, :], shi[:, :], ALU.subtract).then_inc(lo_ready, 1)

            def image(n, a):
                add_x(n - 1, 1 - a, 3)
                add_x(n, a, 0)
                sum_rest(n + 1, 0)
                add_x(n, a, 1)
                sum_rest(n + 1, 1)
                add_x(n, a, 2)

            sum_rest(0, 0)
            sum_rest(0, 1)
            sum_rest(1, 0)
            add_x(0, 0, 0)
            add_x(0, 0, 1)
            sum_rest(1, 1)
            add_x(0, 0, 2)
            with pool.Fori(0, (NI - 2) // 2) as i:
                image(2 * i + 1, 1)
                image(2 * i + 2, 0)
            add_x(NI - 2, 0, 3)
            for g in range(3):
                add_x(NI - 1, 1, g)
            add_x(NI - 1, 1, 3, LAST_PARTS[0])

        @block.scalar
        def _(act):
            act.dma_start(cst[:, :], consts).then_inc(cst_in, 16)
            for k, v in enumerate((gamma, beta, conv_b)):
                act.dma_start(vec[:, k, :], v).then_inc(vec_in, 16)
            act.dma_start(bb[:, :], beta_b.to_broadcast([P, 1])).then_inc(vec_in, 16)

            for ci in range(CT):
                w0, w1, w2 = (wt[:, ci, :, d, :] for d in range(3))
                E, PP, Q, G0, G2, HH = (wtmp[:, k] for k in range(6))
                base = WP * ci
                act.wait_ge(w_pool, base + 3)
                nc.scalar.activation(G0, w0, ACT.Copy, scale=1 / 24).then_inc(w_act, 1)
                nc.scalar.activation(G2, w2, ACT.Copy, scale=1 / 6).then_inc(w_act, 1)
                nc.scalar.activation(HH, w1, ACT.Copy, scale=1 / 12).then_inc(w_act, 1)
                act.wait_ge(w_pool, base + 6)
                act.wait_ge(w_act, WA * ci + 3)
                nc.scalar.activation(w0, w0, ACT.Copy, scale=1 / 4).then_inc(w_act, 1)
                nc.scalar.activation(PP, PP, ACT.Copy, scale=-1 / 6).then_inc(w_act, 1)
                nc.scalar.activation(Q, Q, ACT.Copy, scale=-1 / 6).then_inc(w_act, 1)
                act.wait_ge(w_act, WA * ci + 6)
                act.wait_ge(w_pool, base + 9)
                for k, src in ((0, w0), (5, w2), (1, PP), (2, Q), (3, G2), (4, HH)):
                    nc.scalar.activation(U[:, ci, 0, k], src, ACT.Copy).then_inc(w_act, 1)

            act.wait_ge(grp, 3)
            nc.scalar.activation(tmp[:, 3, :], acc[:, 0, 0:NI * CT], ACT.Sqrt, bias=eps[:, 0:1])\
              .then_inc(root_out, 1)
            act.wait_ge(var_ready, 1)
            nc.scalar.activation(bnv[:, 3, :], bnv[:, 1, :], ACT.Sqrt, scale=1.0 / NI, bias=eps[:, 1:2])\
              .then_inc(root_out, 1)

            def coefficients(m, a):
                src = AB[:, m:m + 1] if isinstance(m, int) else AB[:, bass.ds(m, 1)]
                nc.scalar.activation(ab[:, a:a + 1], src, ACT.Copy).then_inc(ab_ready, 1)
                act.wait_ge(ab_ready, m + 1)

            def signs(m, a, g):
                s = 4 * m + g
                c, h = g % 2, g // 2
                row, rows = rows_of(m, g)
                act.wait_ge(x_in[a][g], arrived(m, a))
                if rows > HR:
                    act.wait_ge(x_in[a][g + 2], arrived(m, a))
                at_least(act, t_ready, 3 * s)
                nc.scalar.activation(
                    u[:, 0:rows, 1:W + 1],
                    xb[:, a, c, :, :].rearrange("p h (r w) -> p (h r) w", w=W)[:, row:row + rows],
                    ACT.Sign, scale=ab[:, a, 0, c:c + 1], bias=ab[:, a, 1, c:c + 1]).then_inc(u_ready, 1)
                at_least(act, cq_done, s)
                at_least(act, aq_done, s)
                act.wait_ge(u_ready, s + 1)
                col = lambda first, step, count: u[:, 0:rows, first:first + 4 * J].rearrange(
                    "p r (j q) -> p q r j", q=4)[:, 0:(count - 1) * step + 1:step]
                view = lambda t: t[:, :, 0:rows * J].rearrange("p q (r j) -> p q r j", j=J)
                nc.scalar.activation(view(T[:, 0:4]), col(2, 1, 4), ACT.Relu, scale=2.0).then_inc(t_ready, 1)
                nc.scalar.activation(view(T4[:, :]), col(0, 1, 4), ACT.Relu, scale=8.0).then_inc(t_ready, 1)
                nc.scalar.activation(view(T[:, 4:6]), col(1, 2, 2), ACT.Relu, scale=4.0).then_inc(t_ready, 1)

            def absolute(m, a, g):
                c, h = g % 2, g // 2
                act.wait_ge(x_in[a][g], arrived(m, a))
                at_least(act, s_ready, 2 * m + h)
                nc.scalar.activation(r[:, c, :], chunk(a, g), ACT.Abs, scale=ab[:, a, 0, c:c + 1],
                                     bias=ab[:, a, 1, c:c + 1]).then_inc(abs_done, 1)
                if c == 1:
                    act.wait_ge(abs_done, 4 * (m - 1) + g + 1)
                    nc.scalar.activation(r[:, c, :], r[:, c, :], ACT.Relu, scale=-1.0, bias=1.0)\
                      .then_inc(q_ready, 1)

            def sum_high(m, h):
                act.wait_ge(s_ready, 2 * m + h + 1)
                at_least(act, cs_done, 2 * m + h)
                nc.scalar.activation(shi[:, :], ssum[:, :], ACT.Copy).then_inc(hi_ready, 1)

            def channel_sums(m):
                act.wait_ge(cs_done, 2 * m + 2)
                at_least(act, crow_in, 128 * m)
                nc.scalar.activation(cs8[:, :], csum[0:2 * SCH, 0:SN], ACT.Copy, bias=float(P))\
                  .then_inc(cs8_ready, 1)

            def evacuate(n, g, part=None):
                s, lo, hi = part or (4 * n + g, 0, N)
                act.wait_ge(m13_done, s + 1)
                at_least(act, sd_done, 2 * s)
                nc.scalar.activation(m13[:, :, lo:hi], acc[:, 0:2, lo:hi], ACT.Copy,
                                     scale=inv_s[:, g % 2:g % 2 + 1]).then_inc(ev13, 1)

            act.wait_ge(coef_ready, 1)
            act.wait_ge(pads, 5)
            coefficients(0, 0)
            signs(0, 0, 0)
            signs(0, 0, 1)
            sum_high(0, 0)
            signs(0, 0, 2)
            signs(0, 0, 3)
            act.wait_ge(scale_ready, 2)

            def image(n, a):
                coefficients(n + 1, 1 - a)
                for g in range(G4):
                    if g == 3:
                        sum_high(n + 1, 1)
                    signs(n + 1, 1 - a, g)
                    evacuate(n, g)
                    if g == 1:
                        sum_high(n + 1, 0)
                    for k in ((0, 1), (2,), (3,), ())[g]:
                        absolute(n + 1, 1 - a, k)
                channel_sums(n + 1)

            evacuate(0, 0)
            sum_high(0, 1)
            coefficients(1, 1)
            signs(1, 1, 0)
            channel_sums(0)
            evacuate(0, 1)
            signs(1, 1, 1)
            absolute(1, 1, 0)
            absolute(1, 1, 1)
            signs(1, 1, 2)
            evacuate(0, 2)
            sum_high(1, 0)
            absolute(1, 1, 2)
            absolute(1, 1, 3)
            signs(1, 1, 3)
            evacuate(0, 3)
            sum_high(1, 1)
            channel_sums(1)
            with act.Fori(0, (NI - 2) // 2) as i:
                image(2 * i + 1, 1)
                image(2 * i + 2, 0)
            for g in range(3):
                evacuate(NI - 1, g)
            for part in LAST_PARTS:
                evacuate(NI - 1, 3, part)

        @block.tensor
        def _(pe):
            pe.wait_ge(wrow, 1)
            for c in range(CT):
                last = nc.tensor.matmul(box[:, c:c + 1], mxb[0:1, c * P:(c + 1) * P], one[:, :],
                                        start=True, stop=True)
            last.then_inc(scale_ready, 1)
            pe.wait_ge(cst_in, 16)
            grouped = cst[:, C_GROUP:C_GROUP + P]
            pe.wait_ge(mv_done, NI // 2)
            nc.tensor.matmul(csum[:, 0:NI * CT], grouped, mv[:, :, :, 0].rearrange("p n c -> p (n c)"),
                             start=True, stop=True).then_inc(grp, 1)
            nc.tensor.matmul(acc[:, 0, 0:NI * CT], grouped, mv[:, :, :, 1].rearrange("p n c -> p (n c)"),
                             start=True, stop=False).then_inc(grp, 1)
            pe.wait_ge(dev_ready, 1)
            nc.tensor.matmul(acc[:, 0, 0:NI * CT], grouped, tmp[:, 1, :], start=False, stop=True)\
              .then_inc(grp, 1)

            def sums(m, h):
                pe.wait_ge(hi_ready, 2 * m + h + 1)
                pe.wait_ge(lo_ready, 2 * m + h + 1)
                if h == 0:
                    at_least(pe, cs8_ready, m)
                    if isinstance(m, int) and m == 0:
                        pe.wait_ge(coef_ready, 1)
                for k in range(SCH):
                    j = SCH * h + k
                    for part in (shi, slo):
                        last = nc.tensor.matmul(
                            csum[0:2 * SCH, 0:SN], sel[:, 7 - j:15 - j], part[:, k * SN:(k + 1) * SN],
                            start=(j == 0 and part is shi), stop=(j == 2 * SCH - 1 and part is slo))
                last.then_inc(cs_done, 1)

            def boxed(n):
                pe.wait_ge(hsum_ready, n + 1)
                at_least(pe, bm_ready, n)
                nc.tensor.matmul(box[:, 0:W], cst[0:H, C_TRI:C_TRI + P], hsum[:, 1, :],
                                 start=True, stop=True).then_inc(box_done, 1)

            def products(n, a, g, pair, part=None):
                h, co = g // 2, g % 2
                s, lo, hi = part or (4 * n + g, 0, N)
                free, count = ((ev13, 1), (sd_done, 2), (y05_done, 1))[pair]
                at_least(pe, free, count * s)
                for b in (2 * pair, 2 * pair + 1):
                    k = BANKS[b]
                    for ci in range(CT):
                        for dy in range(3):
                            at = (HR * h + dy) * J
                            for digits in range(2):
                                last = nc.tensor.matmul(
                                    acc[:, b, lo:hi], U[:, ci, digits, k, dy, co * P:(co + 1) * P],
                                    V[:, a, ci, VPLANE[k], at + lo:at + hi],
                                    start=(ci + dy + digits == 0),
                                    stop=(ci == CT - 1 and dy == 2 and digits == 1))
                last.then_inc((m13_done, m24_done, m05_done)[pair], 1)

            def image(n, a):
                pe.wait_ge(v_ready, 4 * n + 4)
                for g in range(G4):
                    products(n, a, g, 0)
                    if g == 2:
                        sums(n + 1, 0)
                    products(n, a, g, 1)
                    if g == 0:
                        boxed(n)
                    if g == 3:
                        sums(n + 1, 1)
                    products(n, a, g, 2)

            def first_image():
                between = {(0, 0): lambda: sums(0, 0), (1, 0): lambda: sums(0, 1), (1, 2): lambda: boxed(0),
                           (2, 2): lambda: sums(1, 0), (3, 2): lambda: sums(1, 1)}
                for g in range(G4):
                    if g % 2 == 0:
                        pe.wait_ge(v_ready, g + 2)
                    for pair in range(3):
                        products(0, 0, g, pair)
                        if (g, pair) in between:
                            between[g, pair]()

            def last_image():
                n = NI - 1
                pe.wait_ge(v_ready, 4 * n + 4)
                for g in range(G4):
                    for part in (LAST_PARTS if g == 3 else ((4 * n + g, 0, N),)):
                        for pair in range(3):
                            products(n, 1, g, pair, part)
                            if (g, pair) == (0, 1):
                                boxed(n)

            pe.wait_ge(weights_ready, 2 * 2 * CT)
            pe.wait_ge(root_out, 1)
            pe.wait_ge(var_ready, 1)
            first_image()
            with pe.Fori(0, (NI - 2) // 2) as i:
                image(2 * i + 1, 1)
                image(2 * i + 2, 0)
            last_image()

        @block.vector
        def _(dve):
            steps = [0]

            def chain(ins):
                steps[0] += 1
                ins.then_inc(step, 1)
                dve.wait_ge(step, steps[0])

            nc.vector.memset(one[:, :], 1.0).then_inc(pads, 1)
            nc.vector.memset(u[:, :, :], 0.5).then_inc(pads, 1)
            nc.vector.memset(crow[:, :], 0.0).then_inc(pads, 1)
            nc.vector.memset(eps[:, 0:1], GN_EPS)
            nc.vector.memset(eps[:, 1:2], BN_EPS).then_inc(pads, 1)
            for c in range(CT):
                dve.wait_ge(w_in[c], 16)
                chain(nc.vector.tensor_reduce((scl, mxb)[c][:, :], wt[:, c].rearrange("p a b o -> p o (a b)"),
                                              AX.X, ALU.max, apply_absolute_value=True))
            nc.vector.tensor_tensor(scl[:, :], scl[:, :], mxb[:, :], ALU.max).then_inc(wmax, 1)

            def statistics(i):
                for o, a in enumerate((1, 0)):
                    for g in range(G4):
                        c, h = g % 2, g // 2
                        dve.wait_ge(x_in[a][g], 16 * i + 16)
                        for k in range(4):
                            last = nc.vector.bn_stats(st[:, a, c, 4 * h + k], chunk(a, g)[:, k * N:(k + 1) * N])
                        last.then_inc(stats_read, 1)
                    for c in range(CT):
                        dve.wait_ge(stats_read, 8 * i + G4 * o + 3 + c)
                        nc.vector.memset(mark[:, a, c:c + 1], 0.0)
                        nc.vector.bn_aggr(mvt[:, a, c, :], st[:, a, c]).then_inc(aggr_done, 1)
                dve.wait_ge(aggr_done, 4 * i + 4)
                nc.vector.tensor_copy(mv[:, bass.ds(NI - 2 - 2 * i, 2)], mvt[:, :]).then_inc(mv_done, 1)

            statistics(0)
            dve.wait_ge(wall, 1)
            chain(nc.vector.tensor_scalar(mxb[:, :], mxb[:, :], 1e-30, None, ALU.max))
            chain(nc.vector.tensor_scalar(mxb[:, :].bitcast(U32), mxb[:, :].bitcast(U32), 0x7F800000, None,
                                          ALU.bitwise_and))
            chain(nc.vector.reciprocal(scl[:, :], mxb[:, :]))
            chain(nc.vector.tensor_scalar(scl[:, :], scl[:, :], 2.0 ** 14, None, ALU.mult))
            nc.vector.tensor_scalar(mxb[:, :], mxb[:, :], 2.0 ** -14, None, ALU.mult).then_inc(wrow, 1)
            nc.vector.memset(crow[:, 0:1], 0.0).then_inc(wscale, 1)
            dve.wait_ge(scale_ready, 1)
            chain(nc.vector.tensor_copy(inv_s[:, :], box[:, 0:CT]))
            nc.vector.tensor_scalar(neg_inv[:, :], inv_s[:, :], -1.0, None, ALU.mult).then_inc(scale_ready, 1)
            dve.wait_ge(cst_in, 16)
            dve.wait_ge(vec_in, 64)
            nc.vector.tensor_copy(sel[:, :], cst[:, C_SEL:C_SEL + 15]).then_inc(pads, 1)
            chain(nc.vector.tensor_scalar(rcount[:, :], cst[0:H, C_COUNT:C_COUNT + W], float(C), bb[0:H, :],
                                          ALU.mult, ALU.add))
            chain(nc.vector.reciprocal(rcount[:, :], rcount[:, :]))
            with dve.Fori(1, NI // 2) as i:
                statistics(i)

            mean = mv[:, :, :, 0].rearrange("p n c -> p (n c)")
            var = mv[:, :, :, 1].rearrange("p n c -> p (n c)")
            mg, d2, gv, a_, half_sq, d, gm, av = (tmp[:, k, :] for k in range(8))
            mu, vs, bv, rs, bt, off = (bnv[:, k, :] for k in range(6))
            by_c = lambda t: t.rearrange("p (n c) -> p c n", c=CT)
            all_n = lambda t: t[:, :, None].to_broadcast([P, CT, NI])

            def inverse_root(v, s, t, factor):
                chain(nc.vector.reciprocal(s, s))
                chain(nc.vector.scalar_tensor_tensor(out=t, in0=s, scalar=-0.5, in1=s,
                                                     op0=ALU.mult, op1=ALU.mult))
                if factor is not None:
                    nc.vector.tensor_tensor(s, s, factor, ALU.mult)
                chain(nc.vector.tensor_tensor(t, t, v, ALU.mult))
                chain(nc.vector.scalar_tensor_tensor(out=s, in0=t, scalar=1.5, in1=s,
                                                     op0=ALU.add, op1=ALU.mult))

            dve.wait_ge(mv_done, NI // 2)
            dve.wait_ge(grp, 1)
            chain(nc.vector.tensor_tensor(d, mean, csum[:, 0:NI * CT], ALU.subtract))
            nc.vector.tensor_tensor(d2, d, d, ALU.mult).then_inc(dev_ready, 1)
            nc.vector.tensor_copy(mg, csum[:, 0:NI * CT])
            dve.wait_ge(root_out, 1)
            nc.vector.tensor_scalar(gv, acc[:, 0, 0:NI * CT], GN_EPS, None, ALU.add)
            inverse_root(gv, a_, half_sq, None)
            chain(nc.vector.tensor_tensor(gm, a_, d, ALU.mult))
            nc.vector.tensor_tensor(av, a_, a_, ALU.mult)
            chain(nc.vector.tensor_reduce(mu, by_c(gm), AX.X, ALU.add))
            nc.vector.tensor_tensor(av, av, var, ALU.mult)
            chain(nc.vector.scalar_tensor_tensor(out=by_c(gm), in0=all_n(mu), scalar=-1.0 / NI, in1=by_c(gm),
                                                 op0=ALU.mult, op1=ALU.add))
            chain(nc.vector.tensor_tensor(gm, gm, gm, ALU.mult))
            chain(nc.vector.tensor_tensor(gm, gm, av, ALU.add))
            nc.vector.tensor_reduce(vs, by_c(gm), AX.X, ALU.add).then_inc(var_ready, 1)
            dve.wait_ge(var_ready, 1)
            nc.vector.tensor_scalar(bv, vs, 1.0 / NI, BN_EPS, ALU.mult, ALU.add)
            dve.wait_ge(root_out, 2)
            inverse_root(bv, rs, bt, vec[:, 0, :])
            nc.vector.scalar_tensor_tensor(out=off, in0=mu, scalar=-1.0 / NI, in1=rs,
                                           op0=ALU.mult, op1=ALU.mult)
            of_ab = lambda k: AB[:, :, k, :].rearrange("p n c -> p c n")
            chain(nc.vector.tensor_tensor(of_ab(0), by_c(a_), all_n(rs), ALU.mult))
            nc.vector.tensor_tensor(off, off, vec[:, 1, :], ALU.add)
            chain(nc.vector.tensor_tensor(of_ab(1), of_ab(0), by_c(mg), ALU.mult))
            nc.vector.tensor_tensor(of_ab(1), all_n(off), of_ab(1), ALU.subtract).then_inc(coef_ready, 1)

            def transform(m, a, g):
                c, s = g % 2, 4 * m + g
                row, rows = rows_of(m, g)
                at, n = (1 + row) * J, rows * J
                vk = lambda k, count=1: V[:, a, c, VPLANE[k]:VPLANE[k] + count, at:at + n]
                if not (isinstance(m, int) and m == 0):
                    dve.wait_ge(m05_done, 4 * m - 4)
                at_least(dve, v_ready, s)
                dve.wait_ge(t_ready, 3 * s + 2)
                nc.vector.tensor_tensor(cq[:, :, 0:n], T[:, 0:4, 0:n], T4[:, :, 0:n], ALU.subtract)\
                  .then_inc(cq_done, 1)
                dve.wait_ge(t_ready, 3 * s + 3)
                nc.vector.tensor_tensor(aq[:, :, 0:n], T[:, 2:6:3, 0:n], T[:, 0:5:4, 0:n], ALU.subtract)\
                  .then_inc(aq_done, 1)
                dve.wait_ge(cq_done, s + 1)
                nc.vector.tensor_tensor(vk(0, 2), cq[:, 2:4, 0:n], cq[:, 0:2, 0:n], ALU.subtract)
                nc.vector.scalar_tensor_tensor(out=vk(1), in0=cq[:, 2:3, 0:n], scalar=6.0, in1=cq[:, 1:2, 0:n],
                                               op0=ALU.add, op1=ALU.add)
                nc.vector.tensor_tensor(vk(2), cq[:, 2:3, 0:n], cq[:, 1:2, 0:n], ALU.subtract)
                dve.wait_ge(aq_done, s + 1)
                nc.vector.tensor_tensor(vk(3), aq[:, 0:1, 0:n], aq[:, 1:2, 0:n], ALU.add)
                nc.vector.tensor_tensor(vk(4), aq[:, 0:1, 0:n], aq[:, 1:2, 0:n], ALU.subtract)\
                  .then_inc(v_ready, 1)

            def clipped(h):
                for c in range(CT):
                    dve.wait_ge(x_in[0][2 * h + c], arrived(0, 0))
                    nc.vector.tensor_scalar(r[:, c, :], chunk(0, 2 * h + c), AB[:, 0, 0, c:c + 1],
                                            AB[:, 0, 1, c:c + 1], ALU.mult, ALU.add).then_inc(clip, 1)
                for c in range(CT):
                    dve.wait_ge(clip, 5 * h + c + 1)
                    nc.vector.tensor_scalar(r[:, c, :].bitcast(U32), r[:, c, :].bitcast(U32), 0x7FFFFFFF, None,
                                            ALU.bitwise_and).then_inc(clip, 1)
                dve.wait_ge(clip, 5 * h + 4)
                nc.vector.tensor_scalar(r[:, 1, :], r[:, 1, :], 1.0, 1.0, ALU.min, ALU.subtract)\
                  .then_inc(clip, 1)

            def clipped_sum(h):
                dve.wait_ge(clip, 5 * h + 5)
                at_least(dve, lo_ready, h)
                nc.vector.scalar_tensor_tensor(out=ssum[:, :], in0=r[:, 0, :], scalar=1.0, in1=r[:, 1, :],
                                               op0=ALU.min, op1=ALU.add).then_inc(s_ready, 1)

            def pair_sum(m, h):
                dve.wait_ge(abs_done, 4 * (m - 1) + 2 * h + 1)
                dve.wait_ge(q_ready, 2 * (m - 1) + h + 1)
                at_least(dve, lo_ready, 2 * m + h)
                nc.vector.scalar_tensor_tensor(out=ssum[:, :], in0=r[:, 0, :], scalar=1.0, in1=r[:, 1, :],
                                               op0=ALU.min, op1=ALU.subtract).then_inc(s_ready, 1)

            def columns(n):
                dve.wait_ge(crow_in, 128 * n + 128)
                nc.vector.tensor_tensor(hsum[:, 0, :], crow[:, 0:W], crow[:, 1:W + 1], ALU.add)\
                  .then_inc(hpart, 1)
                dve.wait_ge(hpart, n + 1)
                at_least(dve, box_done, n)
                nc.vector.tensor_tensor(hsum[:, 1, :], hsum[:, 0, :], crow[:, 2:W + 2], ALU.add)\
                  .then_inc(hsum_ready, 1)

            def beta_map(n):
                dve.wait_ge(box_done, n + 1)
                at_least(dve, bm_stored, 32 * n)
                nc.vector.scalar_tensor_tensor(
                    out=bm[:, :, :].rearrange("p i j -> p j i"),
                    in0=box[0:H, 0:W].rearrange("p (j i) -> p j i", i=4), scalar=bb[0:H, :],
                    in1=rcount[:, :].rearrange("p (j i) -> p j i", i=4), op0=ALU.add, op1=ALU.mult)\
                  .then_inc(bm_ready, 1)

            def sums_and_differences(n, g, part=None):
                co = g % 2
                s, lo, hi = part or (4 * n + g, 0, N)
                dve.wait_ge(m24_done, s + 1)
                dve.wait_ge(ev13, s + 1)
                for k, scale in ((0, inv_s), (2, neg_inv)):
                    nc.vector.scalar_tensor_tensor(
                        out=sd[:, k:k + 2, lo:hi], in0=acc[:, 2:4, lo:hi], scalar=scale[:, co:co + 1],
                        in1=m13[:, :, lo:hi],
                        op0=ALU.mult, op1=ALU.add).then_inc(sd_done, 1)

            def outputs(n, g, part=None):
                co = g % 2
                s, lo, hi = part or (4 * n + g, 0, N)
                yb, sdb = y[:, g % 2, :, lo:hi], sd[:, :, lo:hi]
                dve.wait_ge(m05_done, s + 1)
                dve.wait_ge(sd_done, 2 * s + 2)
                if not isinstance(n, int) or 2 <= s < G4 * NI:
                    dve.wait_ge(added, s - 1)
                nc.vector.scalar_tensor_tensor(
                    out=yb[:, 0:4:3], in0=acc[:, 4:6, lo:hi], scalar=inv_s[:, co:co + 1], in1=sdb[:, 0:4:2],
                    op0=ALU.mult, op1=ALU.add).then_inc(y05_done, 1)
                nc.vector.scalar_tensor_tensor(out=yb[:, 1], in0=sdb[:, 3], scalar=2.0, in1=sdb[:, 2],
                                               op0=ALU.mult, op1=ALU.add)
                nc.vector.scalar_tensor_tensor(out=yb[:, 2], in0=sdb[:, 1], scalar=4.0, in1=sdb[:, 0],
                                               op0=ALU.mult, op1=ALU.add)
                dve.wait_ge(y05_done, s + 1)
                nc.vector.tensor_tensor(yb[:, 0], yb[:, 0], sdb[:, 1], ALU.add)
                nc.vector.scalar_tensor_tensor(out=yb[:, 3], in0=sdb[:, 3], scalar=8.0, in1=yb[:, 3],
                                               op0=ALU.mult, op1=ALU.add).then_inc(y_done, 1)

            def scale_outputs(n, g, part=None):
                co, h = g % 2, g // 2
                s, lo, hi = part or (4 * n + g, 0, N)
                yb = y[:, g % 2, :, lo:hi]
                dve.wait_ge(y_done, s + 1)
                dve.wait_ge(bmap_in[h], 16 * n + 16)
                nc.vector.scalar_tensor_tensor(
                    out=yb, in0=yb, scalar=vec[:, 2, co:co + 1],
                    in1=bmap[:, h, :].rearrange("p (i n) -> p i n", i=4)[:, :, lo:hi],
                    op0=ALU.add, op1=ALU.mult).then_inc(scaled, 1)

            def finish(n, g):
                outputs(n, g)
                scale_outputs(n, g)

            dve.wait_ge(weights_ready, 2 * 2 * CT)
            dve.wait_ge(coef_ready, 1)
            for h in range(2):
                clipped(h)
                transform(0, 0, 2 * h)
                clipped_sum(h)
                transform(0, 0, 2 * h + 1)

            def image(n, a, prep=True):
                for g in range(G4):
                    if prep and g == 1:
                        pair_sum(n + 1, 0)
                    if g > 0:
                        finish(n, g - 1)
                    else:
                        finish(n - 1, 3)
                        columns(n)
                    if prep:
                        transform(n + 1, 1 - a, g)
                    if g == 0:
                        beta_map(n)
                    if prep or g < 3:
                        sums_and_differences(n, g)
                    if prep and g == 2:
                        pair_sum(n + 1, 1)

            sums_and_differences(0, 0)
            outputs(0, 0)
            transform(1, 1, 0)
            sums_and_differences(0, 1)
            columns(0)
            transform(1, 1, 1)
            outputs(0, 1)
            beta_map(0)
            pair_sum(1, 0)
            transform(1, 1, 2)
            sums_and_differences(0, 2)
            scale_outputs(0, 0)
            scale_outputs(0, 1)
            pair_sum(1, 1)
            outputs(0, 2)
            transform(1, 1, 3)
            scale_outputs(0, 2)
            sums_and_differences(0, 3)
            with dve.Fori(0, (NI - 2) // 2) as i:
                image(2 * i + 1, 1)
                image(2 * i + 2, 0)
            image(NI - 1, 1, prep=False)
            for part in LAST_PARTS:
                sums_and_differences(NI - 1, 3, part)
                outputs(NI - 1, 3, part)
                scale_outputs(NI - 1, 3, part)
            s, lo, hi = LAST_PARTS[1]
            dve.wait_ge(scaled, s + 1)
            xv, yv = x_and_y(1, 3, lo, hi)
            nc.vector.tensor_tensor(xv, xv, yv, ALU.add).then_inc(last_added, 1)


def kernel(x, L0_conv_bn_gamma, L0_conv_bn_beta, L0_conv_conv_w, L0_conv_conv_b, L0_conv_beta_conv_b):
    import numpy as np
    import concourse.bacc as bacc
    from concourse.bass_utils import run_bass_kernel_spmd

    def column(v):
        return np.ascontiguousarray(np.asarray(v).reshape(CT, P).T)

    k = np.arange(P)
    group = (k[:, None] // GROUP == k[None, :] // GROUP).astype(np.float32) / GROUP
    consts = np.zeros((P, C_WIDTH), np.float32)
    consts[:, C_GROUP:C_GROUP + P] = group
    consts[:, C_SEL + 7] = 1.0
    rows = np.arange(H)
    consts[:H, C_TRI:C_TRI + H] = abs(rows[:, None] - rows[None, :]) <= 1
    near = 3.0 - (rows == 0) - (rows == H - 1)
    consts[:H, C_COUNT:C_COUNT + W] = near[:, None] * near[None, :]

    w = np.asarray(L0_conv_conv_w)
    arrays = {
        "x": np.ascontiguousarray(x),
        "w_t": np.ascontiguousarray(w.transpose(1, 2, 3, 0)).reshape(C, 9, C),
        "gamma": column(L0_conv_bn_gamma),
        "beta": column(L0_conv_bn_beta),
        "conv_b": column(L0_conv_conv_b),
        "beta_b": np.asarray(L0_conv_beta_conv_b).reshape(1, 1),
        "consts": consts,
    }
    nc = bacc.Bacc("TRN2", target_bir_lowering=False, num_devices=1)
    args = {name: nc.dram_tensor(name, v.shape, F32, kind="ExternalInput").ap() for name, v in arrays.items()}
    map_rows = nc.dram_tensor("map_rows", (NI, H * W), F32, kind="Internal").ap()
    out = nc.dram_tensor("out", (NI, C, H, W), F32, kind="ExternalOutput").ap()
    conv_preact(nc, args["x"], args["w_t"], args["gamma"], args["beta"], args["conv_b"], args["beta_b"],
                args["consts"], map_rows, out)
    r = run_bass_kernel_spmd(nc, [arrays], core_ids=[0])
    return r.results[0]["out"]
```

```python
from contextlib import ExitStack

import concourse.bass as bass
from concourse import mybir

F32 = mybir.dt.float32
F16 = mybir.dt.float16
U32 = mybir.dt.uint32
ALU = mybir.AluOpType
ACT = mybir.ActivationFunctionType
AX = mybir.AxisListType

P = 128
NI, C, H, W = 16, 256, 56, 56
CT = C // P
HR = H // 2
HPX = HR * W
J = W // 4
N = HR * J
NX = N + J
K6 = 6
G4 = 2 * CT
UP = 60
GROUP = 8
GN_EPS, BN_EPS = 1e-5, 1e-4
SROWS = 7
SN = SROWS * W
SCH = HPX // SN
VPLANE = {0: 0, 5: 1, 1: 2, 2: 3, 3: 4, 4: 5}
BANKS = (1, 3, 2, 4, 0, 5)
C_GROUP, C_SEL, C_TRI, C_COUNT = 0, P, P + 15, P + 15 + P
C_FOLD = C_COUNT + W
C_WIDTH = C_FOLD + 32
SQ = 32
NB = HPX // SQ
LAST_PARTS = ((G4 * NI - 1, 0, N // 2), (G4 * NI, N // 2, N))


def conv_preact(nc, x, w_t, gamma, beta, conv_b, beta_b, consts, sum_rows, map_rows, out):
    x_v = x.rearrange("n (c p) (h r) w -> n c h p (r w)", p=P, h=2)
    out_v = out.rearrange("n (c p) (h r) w -> n c h p (r w)", p=P, h=2)
    x_pairs = x_v[1:NI - 1].rearrange("(i k) c h p f -> i k c h p f", k=2)
    w_v = w_t.rearrange("(c p) t o -> p c (t o)", p=P)

    with ExitStack() as ctx:
        def sb(name, shape, dt=F32):
            return ctx.enter_context(nc.sbuf_tensor(name, shape, dt))

        def sem(name):
            return ctx.enter_context(nc.semaphore(name))

        xb = sb("xb", [P, 2, CT, 2, HPX])
        U = sb("U", [P, CT, 2, K6, 3, C], F16)
        V = sb("V", [P, 2, CT, K6, (H + 2) * J], F16)
        u = sb("u", [P, 2, HR + 1, UP], F16)
        T = sb("T", [P, K6, NX], F16)
        T4 = sb("T4", [P, 4, NX], F16)
        cq = sb("cq", [P, 4, NX], F16)
        aq = sb("aq", [P, 2, NX], F16)
        r = sb("r", [P, CT, HPX + W])
        ssum = sb("ssum", [P, HPX])
        parts = sb("parts", [P, 2, HPX], F16)
        turned = parts[:, :, :].rearrange("p a f -> p (a f)").bitcast(F32)
        quarter = sb("quarter", [P, 2, NB])
        sel = sb("sel", [P, 15], F16)
        bmap = sb("bmap", [P, 2, HPX])
        m13 = sb("m13", [P, 2, N])
        sd = sb("sd", [P, 4, N])
        y = sb("y", [P, 2, 4, N])
        cs8 = sb("cs8", [2 * SCH, SN])
        cs49 = sb("cs49", [NB, 2, SQ])
        crow = sb("crow", [H, W + 2])
        hsum = sb("hsum", [H, 2, W])
        bm = sb("bm", [H, 4, J])
        rcount = sb("rcount", [H, W])
        cst = sb("cst", [P, C_WIDTH])
        vec = sb("vec", [P, 3, CT])
        bb = sb("bb", [P, 1])
        one = sb("one", [1, 1])
        inv_s = sb("inv_s", [P, CT])
        neg_inv = sb("neg_inv", [P, CT])
        st = sb("st", [P, 2, CT, 8, 6])
        mark = sb("mark", [P, 2, CT])
        mvt = sb("mvt", [P, 2, CT, 2])
        mv = sb("mv", [P, NI, CT, 2])
        AB = sb("AB", [P, NI, 2, CT])
        eps = sb("eps", [P, 2])
        ab = sb("ab", [P, 2, 2, CT])
        spare = y[:, :, :, :].rearrange("p a i n -> p (a i n)")
        tmp = spare[:, 0:8 * NI * CT].rearrange("p (k s) -> p k s", k=8)
        bnv = spare[:, 8 * NI * CT:8 * (NI + 1) * CT].rearrange("p (k c) -> p k c", k=8)
        scratch = V[:, :, :, :, :].rearrange("p a c k n -> p (a c k n)").bitcast(F32)
        wt = scratch[:, 0:CT * 9 * C].rearrange("p (c a b o) -> p c a b o", c=CT, a=3, b=3)
        wtmp = scratch[:, CT * 9 * C:CT * 9 * C + 6 * 3 * C].rearrange("p (k a o) -> p k a o", k=6, a=3)
        mxb, scl = (scratch[:, (CT * 9 + 18 + k) * C:(CT * 9 + 18 + k + 1) * C] for k in range(2))

        acc = ctx.enter_context(nc.psum_tensor("acc", [P, K6, 512], F32))
        csum = ctx.enter_context(nc.psum_tensor("csum", [P, 512], F32))
        box = ctx.enter_context(nc.psum_tensor("box", [P, 512], F32))

        w_in = [sem(f"w_in{c}") for c in range(CT)]
        vec_in, cst_in = sem("vec_in"), sem("cst_in")
        x_in = [[sem(f"x_in{a}{g}") for g in range(G4)] for a in range(2)]
        x_out = [[sem(f"x_out{a}{g}") for g in range(G4)] for a in range(2)]
        stats_read, aggr_done, mv_done = sem("stats_read"), sem("aggr_done"), sem("mv_done")
        wmax, wall, wrow, wscale = sem("wmax"), sem("wall"), sem("wrow"), sem("wscale")
        w_pool, w_act, scale_ready = sem("w_pool"), sem("w_act"), sem("scale_ready")
        step, dev_ready, grp = sem("step"), sem("dev_ready"), sem("grp")
        var_ready, root_out, coef_ready = (
            sem(s) for s in ("var_ready", "root_out", "coef_ready"))
        pads, weights_ready = sem("pads"), sem("weights_ready")
        ab_ready, u_ready, u1_ready, t_ready, cq_done, aq_done, v_ready = (
            sem(s) for s in ("ab_ready", "u_ready", "u1_ready", "t_ready", "cq_done", "aq_done", "v_ready"))
        hi_ready, lo_ready = sem("hi_ready"), sem("lo_ready")
        turned_done, quarter_ready = sem("turned_done"), sem("quarter_ready")
        xn_ready, clip, abs_done, q_ready, s_ready, cs_done, cs8_ready, cs_stored, crow_in = (
            sem(s) for s in ("xn_ready", "clip", "abs_done", "q_ready", "s_ready", "cs_done", "cs8_ready",
                             "cs_stored", "crow_in"))
        hpart, hsum_ready, box_done, bm_ready, bm_stored = (
            sem(s) for s in ("hpart", "hsum_ready", "box_done", "bm_ready", "bm_stored"))
        bmap_in = [sem(f"bmap_in{h}") for h in range(2)]
        last_added = sem("last_added")
        m13_done, m24_done, m05_done, ev13, sd_done, y05_done, y_done, scaled, added = (
            sem(s) for s in ("m13_done", "m24_done", "m05_done", "ev13", "sd_done", "y05_done",
                             "y_done", "scaled", "added"))
        pool_scaled = sem("pool_scaled")

        WA = 12
        WP = 15
        STAT_LOADS = 16 * (NI // 2)

        def arrived(n, parity):
            return STAT_LOADS + 8 * (n - parity)

        def at_least(eng, s, value):
            if not (isinstance(value, int) and value <= 0):
                eng.wait_ge(s, value)

        def chunk(a, g):
            return xb[:, a, g % 2, g // 2, :]

        def x_and_y(a, g, lo, hi):
            return (chunk(a, g)[:, 4 * lo:4 * hi].rearrange("p (r j i) -> p r j i", j=J, i=4),
                    y[:, g % 2, :, lo:hi].rearrange("p i (r j) -> p r j i", j=J))

        def rows_of(m, g):
            halo = isinstance(m, int) and m == 0
            return (HR * (g // 2) + halo * (g // 2), HR + (-halo if g // 2 else halo))

        def turned_until(m, h):
            return 2 * m + h - 1

        block = ctx.enter_context(nc.Block())

        @block.sync
        def _(sp):
            def stat_loads(i, even):
                for o, a in enumerate((1, 0)):
                    for g in range(G4):
                        if not isinstance(i, int):
                            sp.wait_ge(stats_read, 8 * i - 8 + G4 * o + g + 1)
                        sp.dma_start(chunk(a, g), x_v[even + a, g % 2, g // 2])\
                          .then_inc(x_in[a][g], 16)

            for c in range(CT):
                sp.dma_start(wt[:, c], w_v[:, c].rearrange("p (a b o) -> p a b o", a=3, b=3)).then_inc(w_in[c], 16)
            stat_loads(0, NI - 2)
            with sp.Fori(1, NI // 2) as i:
                stat_loads(i, i * -2 + (NI - 2))

            def crow_load(m):
                sp.wait_ge(cs8_ready, m + 1)
                if isinstance(m, int) and m == 0:
                    sp.dma_start(sum_rows[m].rearrange("(k f) -> k f", f=SN), cs8[:, :]).then_inc(cs_stored, 16)
                else:
                    sp.dma_start(sum_rows[m].rearrange("(h k f) -> k h f", h=2, f=SQ), cs49[:, :, :])\
                      .then_inc(cs_stored, 16)
                sp.wait_ge(cs_stored, 16 * m + 16)
                at_least(sp, hsum_ready, m)
                sp.dma_start(crow[:, 1:W + 1], sum_rows[m].rearrange("(r w) -> r w", w=W)).then_inc(crow_in, 16)

            def store(n, a, g):
                sp.wait_ge(added, 4 * n + g + 1)
                sp.dma_start(out_v[n, g % 2, g // 2], chunk(a, g)).then_inc(x_out[a][g], 16)

            def load(n, a, g, pair, ahead):
                src = x_v[n] if pair is None else x_pairs[pair + ahead // 2, ahead % 2]
                sp.wait_ge(x_out[a][g], 8 * (n - a))
                sp.dma_start(chunk(a, g), src[g % 2, g // 2]).then_inc(x_in[a][g], 16)

            def image(n, a, loads, last_loads, prep, first=False, pair=None):
                sp.wait_ge(bm_ready, n + 1)
                sp.dma_start(map_rows[n].rearrange("(h i r j) -> h r i j", h=2, i=4, r=HR)[0],
                             bm[0:HR]).then_inc(bm_stored, 16)
                sp.dma_start(map_rows[n].rearrange("(h i r j) -> h r i j", h=2, i=4, r=HR)[1],
                             bm[HR:H]).then_inc(bm_stored, 16)
                sp.wait_ge(bm_stored, 32 * n + 32)
                for h in range(2):
                    if not first:
                        sp.wait_ge(scaled, 2 * n - 1 + h)
                        sp.wait_ge(pool_scaled, 2 * n - 1 + h)
                    sp.dma_start(bmap[:, h, :],
                                 map_rows[bass.ds(n, 1), h * HPX:(h + 1) * HPX].to_broadcast([P, HPX]))\
                      .then_inc(bmap_in[h], 16)
                if not first:
                    store(n - 1, 1 - a, 3)
                    if last_loads:
                        load(n + 1, 1 - a, 3, pair, 2 - a)
                for g in range(3):
                    if prep and g == 2:
                        crow_load(n + 1)
                    store(n, a, g)
                    if loads:
                        load(n + 2, a, g, pair, 3 - a)

            crow_load(0)
            image(0, 0, loads=True, last_loads=False, prep=True, first=True)
            with sp.Fori(0, (NI - 4) // 2) as i:
                image(2 * i + 1, 1, loads=True, last_loads=True, prep=True, pair=i)
                image(2 * i + 2, 0, loads=True, last_loads=True, prep=True, pair=i)
            image(NI - 3, 1, loads=True, last_loads=True, prep=True)
            image(NI - 2, 0, loads=False, last_loads=True, prep=True)
            image(NI - 1, 1, loads=False, last_loads=False, prep=False)
            for (s, lo, hi), ready, value in zip(LAST_PARTS, (added, last_added), (G4 * NI, 1)):
                sp.wait_ge(ready, value)
                sp.dma_start(out_v[NI - 1, 1, 1][:, 4 * lo:4 * hi], chunk(1, 3)[:, 4 * lo:4 * hi])\
                  .then_inc(x_out[1][3], 16)
            for a in range(2):
                for g in range(G4):
                    sp.wait_ge(x_out[a][g], 16 * (NI // 2 + (a == 1 and g == 3)))

        @block.gpsimd
        def _(pool):
            done = [0]

            def after_own():
                pool.wait_ge(w_pool, done[0])

            def signal(ins):
                ins.then_inc(w_pool, 1)
                done[0] += 1

            pool.wait_ge(wmax, 1)
            nc.gpsimd.partition_all_reduce(mxb[:, :], scl[:, :], P, bass.bass_isa.ReduceOp.max)\
              .then_inc(wall, 1)
            pool.wait_ge(wscale, 1)
            for ci in range(CT):
                w0, w1, w2 = (wt[:, ci, :, d, :] for d in range(3))
                E, PP, Q, G0, G2, HH = (wtmp[:, k] for k in range(6))
                for dy in range(3):
                    signal(nc.gpsimd.tensor_tensor(
                        wt[:, ci, dy], wt[:, ci, dy], scl[:, None, :].to_broadcast([P, 3, C]), ALU.mult))
                if ci:
                    pool.wait_ge(w_act, WA * ci)
                after_own()
                signal(nc.gpsimd.tensor_tensor(E, w0, w2, ALU.add))
                after_own()
                signal(nc.gpsimd.tensor_tensor(PP, E, w1, ALU.add))
                signal(nc.gpsimd.tensor_tensor(Q, E, w1, ALU.subtract))
                pool.wait_ge(w_act, WA * ci + 3)
                signal(nc.gpsimd.tensor_tensor(G0, G0, G2, ALU.add))
                after_own()
                signal(nc.gpsimd.tensor_tensor(G2, G0, HH, ALU.add))
                signal(nc.gpsimd.tensor_tensor(HH, G0, HH, ALU.subtract))
                for o, (k, src) in enumerate(((0, w0), (5, w2), (1, PP), (2, Q), (3, G2), (4, HH))):
                    pool.wait_ge(w_act, WA * ci + 6 + o + 1)
                    signal(nc.gpsimd.tensor_tensor(U[:, ci, 1, k], src, U[:, ci, 0, k], ALU.subtract))
            after_own()
            pool.wait_ge(scale_ready, 1)
            for a in range(2):
                for ci in range(CT):
                    for e in (0, (H + 1) * J):
                        last = nc.gpsimd.memset(V[:, a, ci, :, e:e + J], 0.0)
                        last.then_inc(weights_ready, 1)

            def add_x(n, a, g, part=None):
                s, lo, hi = part or (4 * n + g, 0, N)
                if part is not None:
                    pool.wait_ge(scaled, 2 * NI + 1)
                elif g % 2 == 0:
                    pool.wait_ge(scaled, 2 * n + g // 2 + 1)
                else:
                    pool.wait_ge(y_done, s + 1)
                    pool.wait_ge(bmap_in[g // 2], 16 * n + 16)
                    flat = y[:, 1].rearrange("p i n -> p (i n)")
                    nc.gpsimd.tensor_tensor(flat, flat, bmap[:, g // 2, :], ALU.mult).then_inc(pool_scaled, 1)
                    pool.wait_ge(pool_scaled, 2 * n + g // 2 + 1)
                xv, yv = x_and_y(a, g, lo, hi)
                nc.gpsimd.tensor_tensor(xv, xv, yv, ALU.add).then_inc(added, 1)

            def sum_rest(m, h):
                pool.wait_ge(hi_ready, 2 * m + h + 1)
                at_least(pool, cs_done, 2 * m + h)
                nc.gpsimd.tensor_tensor(parts[:, 1], ssum[:, :], parts[:, 0], ALU.subtract).then_inc(lo_ready, 1)

            def image(n, a):
                add_x(n - 1, 1 - a, 3)
                for g in range(3):
                    add_x(n, a, g)

            sum_rest(0, 0)
            sum_rest(0, 1)
            for g in range(3):
                add_x(0, 0, g)
            with pool.Fori(0, (NI - 2) // 2) as i:
                image(2 * i + 1, 1)
                image(2 * i + 2, 0)
            image(NI - 1, 1)
            add_x(NI - 1, 1, 3, LAST_PARTS[0])

        @block.scalar
        def _(act):
            act.dma_start(cst[:, :], consts).then_inc(cst_in, 16)
            for k, v in enumerate((gamma, beta, conv_b)):
                act.dma_start(vec[:, k, :], v).then_inc(vec_in, 16)
            act.dma_start(bb[:, :], beta_b.to_broadcast([P, 1])).then_inc(vec_in, 16)

            for ci in range(CT):
                w0, w1, w2 = (wt[:, ci, :, d, :] for d in range(3))
                E, PP, Q, G0, G2, HH = (wtmp[:, k] for k in range(6))
                base = WP * ci
                act.wait_ge(w_pool, base + 3)
                nc.scalar.activation(G0, w0, ACT.Copy, scale=1 / 24).then_inc(w_act, 1)
                nc.scalar.activation(G2, w2, ACT.Copy, scale=1 / 6).then_inc(w_act, 1)
                nc.scalar.activation(HH, w1, ACT.Copy, scale=1 / 12).then_inc(w_act, 1)
                act.wait_ge(w_pool, base + 6)
                act.wait_ge(w_act, WA * ci + 3)
                nc.scalar.activation(w0, w0, ACT.Copy, scale=1 / 4).then_inc(w_act, 1)
                nc.scalar.activation(PP, PP, ACT.Copy, scale=-1 / 6).then_inc(w_act, 1)
                nc.scalar.activation(Q, Q, ACT.Copy, scale=-1 / 6).then_inc(w_act, 1)
                act.wait_ge(w_act, WA * ci + 6)
                act.wait_ge(w_pool, base + 9)
                for k, src in ((0, w0), (5, w2), (1, PP), (2, Q), (3, G2), (4, HH)):
                    nc.scalar.activation(U[:, ci, 0, k], src, ACT.Copy).then_inc(w_act, 1)

            act.wait_ge(grp, 3)
            nc.scalar.activation(tmp[:, 3, :], acc[:, 0, 0:NI * CT], ACT.Sqrt, bias=eps[:, 0:1])\
              .then_inc(root_out, 1)
            act.wait_ge(var_ready, 1)
            nc.scalar.activation(bnv[:, 3, :], bnv[:, 1, :], ACT.Sqrt, scale=1.0 / NI, bias=eps[:, 1:2])\
              .then_inc(root_out, 1)

            def coefficients(m, a):
                src = AB[:, m:m + 1] if isinstance(m, int) else AB[:, bass.ds(m, 1)]
                nc.scalar.activation(ab[:, a:a + 1], src, ACT.Copy).then_inc(ab_ready, 1)
                act.wait_ge(ab_ready, m + 1)

            def signs(m, a, g):
                s = 4 * m + g
                c, h = g % 2, g // 2
                row, rows = rows_of(m, g)
                act.wait_ge(x_in[a][g], arrived(m, a))
                if rows > HR:
                    act.wait_ge(x_in[a][g + 2], arrived(m, a))
                by_vector = isinstance(m, int) and s == 1
                if not by_vector:
                    at_least(act, t_ready, 3 * s)
                    nc.scalar.activation(
                        u[:, 0, 0:rows, 1:W + 1],
                        xb[:, a, c, :, :].rearrange("p h (r w) -> p (h r) w", w=W)[:, row:row + rows],
                        ACT.Sign, scale=ab[:, a, 0, c:c + 1], bias=ab[:, a, 1, c:c + 1]).then_inc(u_ready, 1)
                at_least(act, cq_done, s)
                at_least(act, aq_done, s)
                if by_vector:
                    act.wait_ge(u1_ready, 1)
                else:
                    act.wait_ge(u_ready, 1 if isinstance(m, int) and s == 0 else s)
                col = lambda first, step, count: u[:, int(by_vector), 0:rows, first:first + 4 * J].rearrange(
                    "p r (j q) -> p q r j", q=4)[:, 0:(count - 1) * step + 1:step]
                view = lambda t: t[:, :, 0:rows * J].rearrange("p q (r j) -> p q r j", j=J)
                nc.scalar.activation(view(T[:, 0:4]), col(2, 1, 4), ACT.Relu, scale=2.0).then_inc(t_ready, 1)
                nc.scalar.activation(view(T4[:, :]), col(0, 1, 4), ACT.Relu, scale=8.0).then_inc(t_ready, 1)
                nc.scalar.activation(view(T[:, 4:6]), col(1, 2, 2), ACT.Relu, scale=4.0).then_inc(t_ready, 1)

            def absolute(m, a, g):
                c, h = g % 2, g // 2
                act.wait_ge(x_in[a][g], arrived(m, a))
                at_least(act, s_ready, 2 * m + h)
                nc.scalar.activation(r[:, c, 0:HPX], chunk(a, g), ACT.Abs, scale=ab[:, a, 0, c:c + 1],
                                     bias=ab[:, a, 1, c:c + 1]).then_inc(abs_done, 1)
                if c == 1:
                    act.wait_ge(abs_done, 4 * (m - 1) + g + 1)
                    nc.scalar.activation(r[:, c, 0:HPX], r[:, c, 0:HPX], ACT.Relu, scale=-1.0, bias=1.0)\
                      .then_inc(q_ready, 1)

            def sum_high(m, h):
                act.wait_ge(s_ready, 2 * m + h + 1)
                at_least(act, cs_done, 2 * m + h)
                nc.scalar.activation(parts[:, 0], ssum[:, :], ACT.Copy).then_inc(hi_ready, 1)

            def channel_sums(m):
                act.wait_ge(cs_done, 2 * m + 2)
                at_least(act, cs_stored, 16 * m)
                if isinstance(m, int) and m == 0:
                    to, of = cs8[:, :], csum[0:2 * SCH, 0:SN]
                else:
                    to, of = cs49[:, :, :].rearrange("p h f -> p (h f)"), csum[0:NB, 0:2 * SQ]
                nc.scalar.activation(to, of, ACT.Copy, bias=float(P)).then_inc(cs8_ready, 1)

            def evacuate(n, g, part=None):
                s, lo, hi = part or (4 * n + g, 0, N)
                act.wait_ge(m13_done, s + 1)
                at_least(act, sd_done, 2 * s)
                scale = inv_s[:, g % 2:g % 2 + 1]
                nc.scalar.activation(m13[:, 0, lo:hi], acc[:, 0, lo:hi], ACT.Identity, scale=scale,
                                     bias=vec[:, 2, g % 2:g % 2 + 1]).then_inc(ev13, 1)
                nc.scalar.activation(m13[:, 1, lo:hi], acc[:, 1, lo:hi], ACT.Copy, scale=scale).then_inc(ev13, 1)

            act.wait_ge(coef_ready, 1)
            act.wait_ge(pads, 5)
            coefficients(0, 0)
            signs(0, 0, 0)
            signs(0, 0, 1)
            signs(0, 0, 2)
            sum_high(0, 0)
            signs(0, 0, 3)
            act.wait_ge(scale_ready, 2)

            def image(n, a):
                coefficients(n + 1, 1 - a)
                for g in range(G4):
                    signs(n + 1, 1 - a, g)
                    evacuate(n, g)
                    for k in ((0, 1), (2,), (3,), ())[g]:
                        absolute(n + 1, 1 - a, k)
                channel_sums(n + 1)

            evacuate(0, 0)
            sum_high(0, 1)
            coefficients(1, 1)
            signs(1, 1, 0)
            channel_sums(0)
            evacuate(0, 1)
            signs(1, 1, 1)
            absolute(1, 1, 0)
            absolute(1, 1, 1)
            signs(1, 1, 2)
            evacuate(0, 2)
            absolute(1, 1, 2)
            absolute(1, 1, 3)
            signs(1, 1, 3)
            evacuate(0, 3)
            channel_sums(1)
            with act.Fori(0, (NI - 2) // 2) as i:
                image(2 * i + 1, 1)
                image(2 * i + 2, 0)
            for g in range(3):
                evacuate(NI - 1, g)
            for part in LAST_PARTS:
                evacuate(NI - 1, 3, part)

        @block.tensor
        def _(pe):
            pe.wait_ge(wrow, 1)
            for c in range(CT):
                last = nc.tensor.matmul(box[:, c:c + 1], mxb[0:1, c * P:(c + 1) * P], one[:, :],
                                        start=True, stop=True)
            last.then_inc(scale_ready, 1)
            pe.wait_ge(cst_in, 16)
            grouped = cst[:, C_GROUP:C_GROUP + P]
            pe.wait_ge(mv_done, NI // 2 - 1)
            pe.wait_ge(aggr_done, 2 * NI)
            nc.tensor.matmul(csum[:, 0:NI * CT], grouped, mv[:, :, :, 0].rearrange("p n c -> p (n c)"),
                             start=True, stop=True).then_inc(grp, 1)
            nc.tensor.matmul(acc[:, 0, 0:NI * CT], grouped, mv[:, :, :, 1].rearrange("p n c -> p (n c)"),
                             start=True, stop=False).then_inc(grp, 1)
            pe.wait_ge(dev_ready, 1)
            nc.tensor.matmul(acc[:, 0, 0:NI * CT], grouped, tmp[:, 1, :], start=False, stop=True)\
              .then_inc(grp, 1)

            def sums(h):
                pe.wait_ge(hi_ready, h + 1)
                pe.wait_ge(lo_ready, h + 1)
                for k in range(SCH):
                    j = SCH * h + k
                    for part in range(2):
                        last = nc.tensor.matmul(
                            csum[0:2 * SCH, 0:SN], sel[:, 7 - j:15 - j], parts[:, part, k * SN:(k + 1) * SN],
                            start=(j + part == 0), stop=(j == 2 * SCH - 1 and part == 1))
                last.then_inc(cs_done, 1)

            def quarter_sums(m, h):
                pe.wait_ge(quarter_ready, turned_until(m, h))
                if h == 0:
                    pe.wait_ge(cs8_ready, m)
                nc.tensor.matmul(csum[0:NB, h * SQ:(h + 1) * SQ], quarter[:, h, :], cst[:, C_FOLD:C_FOLD + SQ],
                                 start=True, stop=True).then_inc(cs_done, 1)

            def boxed(n):
                pe.wait_ge(hsum_ready, n + 1)
                at_least(pe, bm_ready, n)
                nc.tensor.matmul(box[:, 0:W], cst[0:H, C_TRI:C_TRI + P], hsum[:, 1, :],
                                 start=True, stop=True).then_inc(box_done, 1)

            def products(n, a, g, pair, part=None):
                h, co = g // 2, g % 2
                s, lo, hi = part or (4 * n + g, 0, N)
                free, count = ((ev13, 2), (sd_done, 2), (y05_done, 1))[pair]
                at_least(pe, free, count * s)
                for b in (2 * pair, 2 * pair + 1):
                    k = BANKS[b]
                    for ci in range(CT):
                        for dy in range(3):
                            at = (HR * h + dy) * J
                            for digits in range(2):
                                last = nc.tensor.matmul(
                                    acc[:, b, lo:hi], U[:, ci, digits, k, dy, co * P:(co + 1) * P],
                                    V[:, a, ci, VPLANE[k], at + lo:at + hi],
                                    start=(ci + dy + digits == 0),
                                    stop=(ci == CT - 1 and dy == 2 and digits == 1))
                last.then_inc((m13_done, m24_done, m05_done)[pair], 1)

            def image(n, a):
                pe.wait_ge(v_ready, 4 * n + 4)
                for g in range(G4):
                    products(n, a, g, 0)
                    if g == 2:
                        quarter_sums(n + 1, 0)
                    products(n, a, g, 1)
                    if g == 0:
                        boxed(n)
                    if g == 3:
                        quarter_sums(n + 1, 1)
                    products(n, a, g, 2)

            def first_image():
                between = {(0, 1): lambda: sums(0), (1, 0): lambda: sums(1), (1, 2): lambda: boxed(0),
                           (3, 1): lambda: quarter_sums(1, 0), (3, 2): lambda: quarter_sums(1, 1)}
                for g in range(G4):
                    if g % 2 == 0:
                        pe.wait_ge(v_ready, g + 2)
                    for pair in range(3):
                        products(0, 0, g, pair)
                        if (g, pair) in between:
                            between[g, pair]()

            def last_image():
                n = NI - 1
                pe.wait_ge(v_ready, 4 * n + 4)
                for g in range(G4):
                    for part in (LAST_PARTS if g == 3 else ((4 * n + g, 0, N),)):
                        for pair in range(3):
                            products(n, 1, g, pair, part)
                            if (g, pair) == (0, 1):
                                boxed(n)

            pe.wait_ge(weights_ready, 2 * 2 * CT)
            pe.wait_ge(coef_ready, 1)
            pe.wait_ge(root_out, 1)
            pe.wait_ge(var_ready, 1)
            first_image()
            with pe.Fori(0, (NI - 2) // 2) as i:
                image(2 * i + 1, 1)
                image(2 * i + 2, 0)
            last_image()

        @block.vector
        def _(dve):
            steps = [0]

            def chain(ins):
                steps[0] += 1
                ins.then_inc(step, 1)
                dve.wait_ge(step, steps[0])

            nc.vector.memset(one[:, :], 1.0).then_inc(pads, 1)
            nc.vector.memset(u[:, :, :, :], 0.5).then_inc(pads, 1)
            nc.vector.memset(crow[:, :], 0.0).then_inc(pads, 1)
            nc.vector.memset(eps[:, 0:1], GN_EPS)
            nc.vector.memset(eps[:, 1:2], BN_EPS).then_inc(pads, 1)
            for c in range(CT):
                dve.wait_ge(w_in[c], 16)
                chain(nc.vector.tensor_reduce((scl, mxb)[c][:, :], wt[:, c].rearrange("p a b o -> p o (a b)"),
                                              AX.X, ALU.max, apply_absolute_value=True))
            nc.vector.tensor_tensor(scl[:, :], scl[:, :], mxb[:, :], ALU.max).then_inc(wmax, 1)

            def statistics(i, last=False):
                for o, a in enumerate((1, 0)):
                    for g in range(G4):
                        c, h = g % 2, g // 2
                        dve.wait_ge(x_in[a][g], 16 * i + 16)
                        for k in range(4):
                            ins = nc.vector.bn_stats(st[:, a, c, 4 * h + k], chunk(a, g)[:, k * N:(k + 1) * N])
                        ins.then_inc(stats_read, 1)
                    for c in range(CT):
                        dve.wait_ge(stats_read, 8 * i + G4 * o + 3 + c)
                        nc.vector.memset(mark[:, a, c:c + 1], 0.0)
                        nc.vector.bn_aggr(mv[:, a, c, :] if last else mvt[:, a, c, :], st[:, a, c])\
                          .then_inc(aggr_done, 1)
                if not last:
                    dve.wait_ge(aggr_done, 4 * i + 4)
                    nc.vector.tensor_copy(mv[:, bass.ds(NI - 2 - 2 * i, 2)], mvt[:, :]).then_inc(mv_done, 1)

            statistics(0)
            dve.wait_ge(wall, 1)
            chain(nc.vector.tensor_scalar(mxb[:, :], mxb[:, :], 1e-30, None, ALU.max))
            chain(nc.vector.tensor_scalar(mxb[:, :].bitcast(U32), mxb[:, :].bitcast(U32), 0x7F800000, None,
                                          ALU.bitwise_and))
            chain(nc.vector.reciprocal(scl[:, :], mxb[:, :]))
            chain(nc.vector.tensor_scalar(scl[:, :], scl[:, :], 2.0 ** 14, None, ALU.mult))
            nc.vector.tensor_scalar(mxb[:, :], mxb[:, :], 2.0 ** -14, None, ALU.mult).then_inc(wrow, 1)
            nc.vector.memset(crow[:, 0:1], 0.0).then_inc(wscale, 1)
            dve.wait_ge(scale_ready, 1)
            chain(nc.vector.tensor_copy(inv_s[:, :], box[:, 0:CT]))
            nc.vector.tensor_scalar(neg_inv[:, :], inv_s[:, :], -1.0, None, ALU.mult).then_inc(scale_ready, 1)
            dve.wait_ge(cst_in, 16)
            dve.wait_ge(vec_in, 64)
            nc.vector.tensor_copy(sel[:, :], cst[:, C_SEL:C_SEL + 15]).then_inc(pads, 1)
            chain(nc.vector.tensor_scalar(rcount[:, :], cst[0:H, C_COUNT:C_COUNT + W], float(C), bb[0:H, :],
                                          ALU.mult, ALU.add))
            chain(nc.vector.reciprocal(rcount[:, :], rcount[:, :]))
            with dve.Fori(1, NI // 2 - 1) as i:
                statistics(i)
            statistics(NI // 2 - 1, last=True)

            mean = mv[:, :, :, 0].rearrange("p n c -> p (n c)")
            var = mv[:, :, :, 1].rearrange("p n c -> p (n c)")
            mg, d2, gv, a_, half_sq, d, gm, av = (tmp[:, k, :] for k in range(8))
            mu, vs, bv, rs, bt, off = (bnv[:, k, :] for k in range(6))
            by_c = lambda t: t.rearrange("p (n c) -> p c n", c=CT)
            all_n = lambda t: t[:, :, None].to_broadcast([P, CT, NI])

            def inverse_root(v, s, t, factor):
                chain(nc.vector.reciprocal(s, s))
                chain(nc.vector.scalar_tensor_tensor(out=t, in0=s, scalar=-0.5, in1=s,
                                                     op0=ALU.mult, op1=ALU.mult))
                if factor is not None:
                    nc.vector.tensor_tensor(s, s, factor, ALU.mult)
                chain(nc.vector.tensor_tensor(t, t, v, ALU.mult))
                chain(nc.vector.scalar_tensor_tensor(out=s, in0=t, scalar=1.5, in1=s,
                                                     op0=ALU.add, op1=ALU.mult))

            dve.wait_ge(mv_done, NI // 2 - 1)
            dve.wait_ge(aggr_done, 2 * NI)
            dve.wait_ge(grp, 1)
            chain(nc.vector.tensor_tensor(d, mean, csum[:, 0:NI * CT], ALU.subtract))
            nc.vector.tensor_tensor(d2, d, d, ALU.mult).then_inc(dev_ready, 1)
            nc.vector.tensor_copy(mg, csum[:, 0:NI * CT])
            dve.wait_ge(root_out, 1)
            nc.vector.tensor_scalar(gv, acc[:, 0, 0:NI * CT], GN_EPS, None, ALU.add)
            inverse_root(gv, a_, half_sq, None)
            chain(nc.vector.tensor_tensor(gm, a_, d, ALU.mult))
            nc.vector.tensor_tensor(av, a_, a_, ALU.mult)
            chain(nc.vector.tensor_reduce(mu, by_c(gm), AX.X, ALU.add))
            nc.vector.tensor_tensor(av, av, var, ALU.mult)
            chain(nc.vector.scalar_tensor_tensor(out=by_c(gm), in0=all_n(mu), scalar=-1.0 / NI, in1=by_c(gm),
                                                 op0=ALU.mult, op1=ALU.add))
            chain(nc.vector.tensor_tensor(gm, gm, gm, ALU.mult))
            chain(nc.vector.tensor_tensor(gm, gm, av, ALU.add))
            nc.vector.tensor_reduce(vs, by_c(gm), AX.X, ALU.add).then_inc(var_ready, 1)
            dve.wait_ge(var_ready, 1)
            nc.vector.tensor_scalar(bv, vs, 1.0 / NI, BN_EPS, ALU.mult, ALU.add)
            dve.wait_ge(root_out, 2)
            inverse_root(bv, rs, bt, vec[:, 0, :])
            nc.vector.scalar_tensor_tensor(out=off, in0=mu, scalar=-1.0 / NI, in1=rs,
                                           op0=ALU.mult, op1=ALU.mult)
            of_ab = lambda k: AB[:, :, k, :].rearrange("p n c -> p c n")
            chain(nc.vector.tensor_tensor(of_ab(0), by_c(a_), all_n(rs), ALU.mult))
            nc.vector.tensor_tensor(off, off, vec[:, 1, :], ALU.add)
            chain(nc.vector.tensor_tensor(of_ab(1), of_ab(0), by_c(mg), ALU.mult))
            nc.vector.tensor_tensor(of_ab(1), all_n(off), of_ab(1), ALU.subtract).then_inc(coef_ready, 1)

            def transform(m, a, g):
                c, s = g % 2, 4 * m + g
                row, rows = rows_of(m, g)
                at, n = (1 + row) * J, rows * J
                vk = lambda k, count=1: V[:, a, c, VPLANE[k]:VPLANE[k] + count, at:at + n]
                if not (isinstance(m, int) and m == 0):
                    dve.wait_ge(m05_done, 4 * m - 4)
                at_least(dve, v_ready, s)
                dve.wait_ge(t_ready, 3 * s + 2)
                nc.vector.tensor_tensor(cq[:, :, 0:n], T[:, 0:4, 0:n], T4[:, :, 0:n], ALU.subtract)\
                  .then_inc(cq_done, 1)
                dve.wait_ge(t_ready, 3 * s + 3)
                nc.vector.tensor_tensor(aq[:, :, 0:n], T[:, 2:6:3, 0:n], T[:, 0:5:4, 0:n], ALU.subtract)\
                  .then_inc(aq_done, 1)
                dve.wait_ge(cq_done, s + 1)
                nc.vector.tensor_tensor(vk(0, 2), cq[:, 2:4, 0:n], cq[:, 0:2, 0:n], ALU.subtract)
                nc.vector.scalar_tensor_tensor(out=vk(1), in0=cq[:, 2:3, 0:n], scalar=6.0, in1=cq[:, 1:2, 0:n],
                                               op0=ALU.add, op1=ALU.add)
                nc.vector.tensor_tensor(vk(2), cq[:, 2:3, 0:n], cq[:, 1:2, 0:n], ALU.subtract)
                dve.wait_ge(aq_done, s + 1)
                nc.vector.tensor_tensor(vk(3), aq[:, 0:1, 0:n], aq[:, 1:2, 0:n], ALU.add)
                nc.vector.tensor_tensor(vk(4), aq[:, 0:1, 0:n], aq[:, 1:2, 0:n], ALU.subtract)\
                  .then_inc(v_ready, 1)

            def normalized(h):
                at_least(dve, s_ready, h)
                for c in (1, 0):
                    with_signs = h == 0 and c == 1
                    count = HPX + (W if with_signs else 0)
                    for part in (h, 1) if with_signs else (h,):
                        dve.wait_ge(x_in[0][2 * part + c], arrived(0, 0))
                    nc.vector.tensor_scalar(
                        r[:, c, 0:count], xb[:, 0, c, :, :].rearrange("p h f -> p (h f)")[:, h * HPX:h * HPX + count],
                        AB[:, 0, 0, c:c + 1], AB[:, 0, 1, c:c + 1], ALU.mult, ALU.add).then_inc(xn_ready, 1)
                    if with_signs:
                        dve.wait_ge(xn_ready, 1)
                        nc.vector.tensor_scalar(u[:, 1, :, 1:W + 1], r[:, 1, :].rearrange("p (r w) -> p r w", w=W),
                                                0.0, None, ALU.is_gt).then_inc(u1_ready, 1)

            def magnitudes(h):
                dve.wait_ge(xn_ready, 2 * h + 2)
                for c in (1, 0):
                    nc.vector.tensor_scalar(r[:, c, 0:HPX].bitcast(U32), r[:, c, 0:HPX].bitcast(U32), 0x7FFFFFFF,
                                            None, ALU.bitwise_and).then_inc(clip, 1)

            def clipped(h):
                dve.wait_ge(clip, 3 * h + 1)
                nc.vector.tensor_scalar(r[:, 1, 0:HPX], r[:, 1, 0:HPX], 1.0, 1.0, ALU.min, ALU.subtract)\
                  .then_inc(clip, 1)

            def clipped_sum(h):
                dve.wait_ge(clip, 3 * h + 3)
                at_least(dve, lo_ready, h)
                nc.vector.scalar_tensor_tensor(out=ssum[:, :], in0=r[:, 0, 0:HPX], scalar=1.0, in1=r[:, 1, 0:HPX],
                                               op0=ALU.min, op1=ALU.add).then_inc(s_ready, 1)

            def pair_sum(m, h):
                dve.wait_ge(abs_done, 4 * (m - 1) + 2 * h + 1)
                dve.wait_ge(q_ready, 2 * (m - 1) + h + 1)
                if isinstance(m, int) and m == 1 and h == 0:
                    dve.wait_ge(lo_ready, 2)
                else:
                    dve.wait_ge(turned_done, turned_until(m, h) - 1)
                nc.vector.scalar_tensor_tensor(out=ssum[:, :], in0=r[:, 0, 0:HPX], scalar=1.0, in1=r[:, 1, 0:HPX],
                                               op0=ALU.min, op1=ALU.subtract).then_inc(s_ready, 1)

            def turn(m, h):
                dve.wait_ge(s_ready, 2 * m + h + 1)
                if h == 0:
                    dve.wait_ge(cs_done, 2 * m)
                else:
                    dve.wait_ge(quarter_ready, turned_until(m, 0))
                nc.vector.transpose(turned.bitcast(U32), ssum[:, :].bitcast(U32)).then_inc(turned_done, 1)
                dve.wait_ge(turned_done, turned_until(m, h))
                nc.vector.tensor_reduce(quarter[:, h, :], turned.rearrange("p (b i) -> p b i", i=SQ), AX.X, ALU.add)\
                  .then_inc(quarter_ready, 1)

            def columns(n):
                dve.wait_ge(crow_in, 16 * n + 16)
                nc.vector.tensor_tensor(hsum[:, 0, :], crow[:, 0:W], crow[:, 1:W + 1], ALU.add)\
                  .then_inc(hpart, 1)
                dve.wait_ge(hpart, n + 1)
                at_least(dve, box_done, n)
                nc.vector.tensor_tensor(hsum[:, 1, :], hsum[:, 0, :], crow[:, 2:W + 2], ALU.add)\
                  .then_inc(hsum_ready, 1)

            def beta_map(n):
                dve.wait_ge(box_done, n + 1)
                at_least(dve, bm_stored, 32 * n)
                nc.vector.scalar_tensor_tensor(
                    out=bm[:, :, :].rearrange("p i j -> p j i"),
                    in0=box[0:H, 0:W].rearrange("p (j i) -> p j i", i=4), scalar=bb[0:H, :],
                    in1=rcount[:, :].rearrange("p (j i) -> p j i", i=4), op0=ALU.add, op1=ALU.mult)\
                  .then_inc(bm_ready, 1)

            def sums_and_differences(n, g, part=None):
                co = g % 2
                s, lo, hi = part or (4 * n + g, 0, N)
                at_least(dve, y_done, s)
                dve.wait_ge(m24_done, s + 1)
                dve.wait_ge(ev13, 2 * s + 2)
                for k, scale in ((0, inv_s), (2, neg_inv)):
                    nc.vector.scalar_tensor_tensor(
                        out=sd[:, k:k + 2, lo:hi], in0=acc[:, 2:4, lo:hi], scalar=scale[:, co:co + 1],
                        in1=m13[:, :, lo:hi],
                        op0=ALU.mult, op1=ALU.add).then_inc(sd_done, 1)

            def outputs(n, g, part=None):
                co = g % 2
                s, lo, hi = part or (4 * n + g, 0, N)
                yb, sdb = y[:, g % 2, :, lo:hi], sd[:, :, lo:hi]
                dve.wait_ge(m05_done, s + 1)
                dve.wait_ge(sd_done, 2 * s + 2)
                if not isinstance(n, int) or 2 <= s < G4 * NI:
                    dve.wait_ge(added, s - 1)
                nc.vector.scalar_tensor_tensor(
                    out=yb[:, 0:4:3], in0=acc[:, 4:6, lo:hi], scalar=inv_s[:, co:co + 1], in1=sdb[:, 0:4:2],
                    op0=ALU.mult, op1=ALU.add).then_inc(y05_done, 1)
                nc.vector.scalar_tensor_tensor(out=yb[:, 1], in0=sdb[:, 3], scalar=2.0, in1=sdb[:, 2],
                                               op0=ALU.mult, op1=ALU.add)
                nc.vector.scalar_tensor_tensor(out=yb[:, 2], in0=sdb[:, 1], scalar=4.0, in1=sdb[:, 0],
                                               op0=ALU.mult, op1=ALU.add)
                dve.wait_ge(y05_done, s + 1)
                nc.vector.tensor_tensor(yb[:, 0], yb[:, 0], sdb[:, 1], ALU.add)
                nc.vector.scalar_tensor_tensor(out=yb[:, 3], in0=sdb[:, 3], scalar=8.0, in1=yb[:, 3],
                                               op0=ALU.mult, op1=ALU.add).then_inc(y_done, 1)

            def scale_outputs(n, g, part=None):
                h = g // 2
                s, lo, hi = part or (4 * n + g, 0, N)
                yb = y[:, g % 2, :, lo:hi]
                dve.wait_ge(y_done, s + 1)
                dve.wait_ge(bmap_in[h], 16 * n + 16)
                nc.vector.tensor_tensor(yb, yb, bmap[:, h, :].rearrange("p (i n) -> p i n", i=4)[:, :, lo:hi],
                                        ALU.mult).then_inc(scaled, 1)

            def finish(n, g):
                outputs(n, g)
                if g % 2 == 0:
                    scale_outputs(n, g)

            dve.wait_ge(weights_ready, 2 * 2 * CT)
            dve.wait_ge(coef_ready, 1)
            normalized(0)
            transform(0, 0, 0)
            magnitudes(0)
            transform(0, 0, 1)
            clipped(0)
            clipped_sum(0)
            normalized(1)
            magnitudes(1)
            clipped(1)
            transform(0, 0, 2)
            clipped_sum(1)
            transform(0, 0, 3)

            def image(n, a, prep=True):
                for g in range(G4):
                    if g == 0:
                        finish(n - 1, 3)
                        columns(n)
                    elif prep and g == 3:
                        outputs(n, 2)
                        turn(n + 1, 1)
                        scale_outputs(n, 2)
                    else:
                        finish(n, g - 1)
                    if prep:
                        transform(n + 1, 1 - a, g)
                    if g == 0:
                        beta_map(n)
                    if prep and g == 1:
                        turn(n + 1, 0)
                    if prep or g < 3:
                        sums_and_differences(n, g)
                    if prep and g % 2 == 0:
                        pair_sum(n + 1, g // 2)

            sums_and_differences(0, 0)
            outputs(0, 0)
            transform(1, 1, 0)
            sums_and_differences(0, 1)
            columns(0)
            transform(1, 1, 1)
            outputs(0, 1)
            beta_map(0)
            pair_sum(1, 0)
            transform(1, 1, 2)
            sums_and_differences(0, 2)
            scale_outputs(0, 0)
            turn(1, 0)
            pair_sum(1, 1)
            outputs(0, 2)
            transform(1, 1, 3)
            turn(1, 1)
            scale_outputs(0, 2)
            sums_and_differences(0, 3)
            with dve.Fori(0, (NI - 2) // 2) as i:
                image(2 * i + 1, 1)
                image(2 * i + 2, 0)
            image(NI - 1, 1, prep=False)
            for part in LAST_PARTS:
                sums_and_differences(NI - 1, 3, part)
                outputs(NI - 1, 3, part)
                scale_outputs(NI - 1, 3, part)
            s, lo, hi = LAST_PARTS[1]
            dve.wait_ge(scaled, 2 * NI + 2)
            xv, yv = x_and_y(1, 3, lo, hi)
            nc.vector.tensor_tensor(xv, xv, yv, ALU.add).then_inc(last_added, 1)


def kernel(x, L0_conv_bn_gamma, L0_conv_bn_beta, L0_conv_conv_w, L0_conv_conv_b, L0_conv_beta_conv_b):
    import numpy as np
    import concourse.bacc as bacc
    from concourse.bass_utils import run_bass_kernel_spmd

    def column(v):
        return np.ascontiguousarray(np.asarray(v).reshape(CT, P).T)

    k = np.arange(P)
    group = (k[:, None] // GROUP == k[None, :] // GROUP).astype(np.float32) / GROUP
    consts = np.zeros((P, C_WIDTH), np.float32)
    consts[:, C_GROUP:C_GROUP + P] = group
    consts[:, C_SEL + 7] = 1.0
    consts[k, C_FOLD + k % SQ] = 1.0
    rows = np.arange(H)
    consts[:H, C_TRI:C_TRI + H] = abs(rows[:, None] - rows[None, :]) <= 1
    near = 3.0 - (rows == 0) - (rows == H - 1)
    consts[:H, C_COUNT:C_COUNT + W] = near[:, None] * near[None, :]

    w = np.asarray(L0_conv_conv_w)
    arrays = {
        "x": np.ascontiguousarray(x),
        "w_t": np.ascontiguousarray(w.transpose(1, 2, 3, 0)).reshape(C, 9, C),
        "gamma": column(L0_conv_bn_gamma),
        "beta": column(L0_conv_bn_beta),
        "conv_b": column(L0_conv_conv_b),
        "beta_b": np.asarray(L0_conv_beta_conv_b).reshape(1, 1),
        "consts": consts,
    }
    nc = bacc.Bacc("TRN2", target_bir_lowering=False, num_devices=1)
    args = {name: nc.dram_tensor(name, v.shape, F32, kind="ExternalInput").ap() for name, v in arrays.items()}
    sum_rows = nc.dram_tensor("sum_rows", (NI, H * W), F32, kind="Internal").ap()
    map_rows = nc.dram_tensor("map_rows", (NI, H * W), F32, kind="Internal").ap()
    out = nc.dram_tensor("out", (NI, C, H, W), F32, kind="ExternalOutput").ap()
    conv_preact(nc, args["x"], args["w_t"], args["gamma"], args["beta"], args["conv_b"], args["beta_b"],
                args["consts"], sum_rows, map_rows, out)
    r = run_bass_kernel_spmd(nc, [arrays], core_ids=[0])
    return r.results[0]["out"]
```
